# Optimizing a Trainium2 kernel written in Bass

```python
import numpy as np
import jax
import jax.numpy as jnp

def _softmax(x, axis=-1):
    return jax.nn.softmax(x, axis=axis)

def _gelu(x):
    return jax.nn.gelu(x, approximate=True)

def _silu(x):
    return jax.nn.silu(x)

def _sigmoid(x):
    return jax.nn.sigmoid(x)

def _layernorm(x, axis=-1, eps=1e-05):
    m = jnp.mean(x, axis=axis, keepdims=True)
    v = jnp.var(x, axis=axis, keepdims=True)
    return (x - m) / jnp.sqrt(v + eps)

def _scatter_add(tgt, idx, src, axis=0):
    return tgt.at[idx].add(src)

def _segment_sum(src, seg, n):
    return jax.ops.segment_sum(src, seg, n)
kernel_name = 'mk_adaln_ffn_d1_seqx_r4_0e0580'

def setup_inputs(seed: int=0):
    np.random.seed(seed)
    _w = jnp.asarray

    def _rec_inputs():
        import jax
        import jax.numpy as jnp
        _rk = jax.random.key(seed)
        x = -8.015e-05 + 0.9999 * jax.random.normal(jax.random.fold_in(_rk, 1), (128, 64, 512), jnp.float32)
        _lenS = 64 - jax.random.randint(jax.random.fold_in(_rk, 7), (128,), 0, max(1, 64 // 4) + 1, jnp.int32)
        _lenS2 = 64 - jax.random.randint(jax.random.fold_in(_rk, 8), (128,), 0, max(1, 64 // 4) + 1, jnp.int32)
        cond_1024 = 0.00191187 + 0.999416 * jax.random.normal(jax.random.fold_in(_rk, 11), (128, 256), jnp.float32)
        return (x, cond_1024)
    x, cond_1024 = _rec_inputs()

    def _L0_cond_setup():
        import jax, jax.numpy as jnp
        import numpy as np
        B, N, V_DIM, Q_DIM = (64, 100, 512, 256)
        key = jax.random.key(seed)
        k1, k2, k3, k4 = jax.random.split(key, 4)
        v = jax.random.normal(k1, (B, N, V_DIM), dtype=jnp.float32)
        q = jax.random.normal(k2, (B, Q_DIM), dtype=jnp.float32)
        W3 = jax.random.normal(k3, (Q_DIM, V_DIM), dtype=jnp.float32) * (1.0 / np.sqrt(Q_DIM))
        b3 = jnp.zeros((V_DIM,), dtype=jnp.float32)
        W2 = jax.random.normal(k4, (V_DIM, V_DIM), dtype=jnp.float32) * (1.0 / np.sqrt(V_DIM))
        b2 = jnp.zeros((V_DIM,), dtype=jnp.float32)
        return {'v': v, 'q': q, 'W3': W3, 'b3': b3, 'W2': W2, 'b2': b2}
    _L0_cond_all = _L0_cond_setup()
    _L0_cond_in = {k: v for k, v in _L0_cond_all.items() if k in ('W3', 'b3', 'W2', 'b2')}
    del _L0_cond_all

    def _L0_ffn_setup():
        import jax, jax.numpy as jnp
        import numpy as np
        E, K, H, I = (64, 6, 512, 352)
        NS = 2
        IS = NS * I
        CAP = 64
        T_TOKENS = (1, 256)
        SCALE = 0.02

        def _moe_infer(x, gate_w, w_gate, w_up, w_down):
            T = x.shape[0]
            TK = T * K
            logits = x @ gate_w.T
            scores = jax.nn.softmax(logits, axis=-1)
            topk_w, topk_i = jax.lax.top_k(scores, K)
            flat_i = topk_i.reshape(-1)
            flat_w = topk_w.reshape(-1)
            token_ids = jnp.arange(TK, dtype=jnp.int32) // K
            order = jnp.argsort(flat_i)
            sorted_e = flat_i[order]
            counts = jnp.bincount(flat_i, length=E)
            starts = jnp.concatenate([jnp.zeros((1,), counts.dtype), jnp.cumsum(counts)[:-1]])
            pos_sorted = jnp.arange(TK) - starts[sorted_e]
            pos = jnp.zeros((TK,), jnp.int32).at[order].set(pos_sorted.astype(jnp.int32))
            valid = pos < CAP
            slot = jnp.where(valid, pos, CAP)
            buf = jnp.zeros((E, CAP + 1, H), x.dtype).at[flat_i, slot].set(x[token_ids])
            g = jnp.einsum('ech,ehi->eci', buf, w_gate)
            u = jnp.einsum('ech,ehi->eci', buf, w_up)
            y = jnp.einsum('eci,eih->ech', jax.nn.silu(g) * u, w_down)
            out_slots = y[flat_i, slot] * (flat_w * valid)[:, None]
            return out_slots.reshape(T, K, H).sum(axis=1)
        key = jax.random.key(seed)
        ks = jax.random.split(key, 8)
        f32 = jnp.float32
        return {'hidden_states': jax.random.normal(ks[0], (*T_TOKENS, H), f32), 'gate_w': jax.random.normal(ks[1], (E, H), f32) * SCALE, 'w_gate': jax.random.normal(ks[2], (E, H, I), f32) * SCALE, 'w_up': jax.random.normal(ks[3], (E, H, I), f32) * SCALE, 'w_down': jax.random.normal(ks[4], (E, I, H), f32) * SCALE, 'sw_gate': jax.random.normal(ks[5], (H, IS), f32) * SCALE, 'sw_up': jax.random.normal(ks[6], (H, IS), f32) * SCALE, 'sw_down': jax.random.normal(ks[7], (IS, H), f32) * SCALE}
    _L0_ffn_all = _L0_ffn_setup()
    _L0_ffn_in = {k: v for k, v in _L0_ffn_all.items() if k in ('gate_w', 'w_gate', 'w_up', 'w_down', 'sw_gate', 'sw_up', 'sw_down')}
    del _L0_ffn_all
    return {'x': x, 'cond_1024': cond_1024, 'L0_cond_W3': _L0_cond_in['W3'], 'L0_cond_b3': _L0_cond_in['b3'], 'L0_cond_W2': _L0_cond_in['W2'], 'L0_cond_b2': _L0_cond_in['b2'], 'L0_ffn_gate_w': _L0_ffn_in['gate_w'], 'L0_ffn_w_gate': _L0_ffn_in['w_gate'], 'L0_ffn_w_up': _L0_ffn_in['w_up'], 'L0_ffn_w_down': _L0_ffn_in['w_down'], 'L0_ffn_sw_gate': _L0_ffn_in['sw_gate'], 'L0_ffn_sw_up': _L0_ffn_in['sw_up'], 'L0_ffn_sw_down': _L0_ffn_in['sw_down']}

def reference(x, cond_1024, L0_cond_W3, L0_cond_b3, L0_cond_W2, L0_cond_b2, L0_ffn_gate_w, L0_ffn_w_gate, L0_ffn_w_up, L0_ffn_w_down, L0_ffn_sw_gate, L0_ffn_sw_up, L0_ffn_sw_down):
    import jax
    import jax.numpy as jnp

    def _L0_cond_ref(v, q, W3, b3, W2, b2):
        import jax, jax.numpy as jnp
        import numpy as np
        B, N, V_DIM, Q_DIM = (64, 100, 512, 256)
        q_emb = jax.nn.relu(q @ W3 + b3)
        n = v.shape[1]
        v_sum = jnp.sum(v, axis=1, keepdims=True)
        x = (n * v + v_sum) * q_emb[:, None, :]
        return jax.nn.relu(x @ W2 + b2)

    def _L0_ffn_ref(hidden_states, gate_w, w_gate, w_up, w_down, sw_gate, sw_up, sw_down):
        import jax, jax.numpy as jnp
        import numpy as np
        E, K, H, I = (64, 6, 512, 352)
        NS = 2
        IS = NS * I
        CAP = 64
        T_TOKENS = (1, 256)
        SCALE = 0.02

        def _moe_infer(x, gate_w, w_gate, w_up, w_down):
            T = x.shape[0]
            TK = T * K
            logits = x @ gate_w.T
            scores = jax.nn.softmax(logits, axis=-1)
            topk_w, topk_i = jax.lax.top_k(scores, K)
            flat_i = topk_i.reshape(-1)
            flat_w = topk_w.reshape(-1)
            token_ids = jnp.arange(TK, dtype=jnp.int32) // K
            order = jnp.argsort(flat_i)
            sorted_e = flat_i[order]
            counts = jnp.bincount(flat_i, length=E)
            starts = jnp.concatenate([jnp.zeros((1,), counts.dtype), jnp.cumsum(counts)[:-1]])
            pos_sorted = jnp.arange(TK) - starts[sorted_e]
            pos = jnp.zeros((TK,), jnp.int32).at[order].set(pos_sorted.astype(jnp.int32))
            valid = pos < CAP
            slot = jnp.where(valid, pos, CAP)
            buf = jnp.zeros((E, CAP + 1, H), x.dtype).at[flat_i, slot].set(x[token_ids])
            g = jnp.einsum('ech,ehi->eci', buf, w_gate)
            u = jnp.einsum('ech,ehi->eci', buf, w_up)
            y = jnp.einsum('eci,eih->ech', jax.nn.silu(g) * u, w_down)
            out_slots = y[flat_i, slot] * (flat_w * valid)[:, None]
            return out_slots.reshape(T, K, H).sum(axis=1)
        orig_shape = hidden_states.shape
        x = hidden_states.reshape(-1, orig_shape[-1])
        y = _moe_infer(x, gate_w, w_gate, w_up, w_down).reshape(orig_shape)
        shared = jax.nn.silu(hidden_states @ sw_gate) * (hidden_states @ sw_up) @ sw_down
        return y + shared
    x = x + _L0_ffn_ref(_L0_cond_ref(x, cond_1024, L0_cond_W3, L0_cond_b3, L0_cond_W2, L0_cond_b2), L0_ffn_gate_w, L0_ffn_w_gate, L0_ffn_w_up, L0_ffn_w_down, L0_ffn_sw_gate, L0_ffn_sw_up, L0_ffn_sw_down)
    return x

_drawn_inputs = setup_inputs


def setup_inputs(seed=0):
    import zlib

    import numpy as np

    out = dict(_drawn_inputs(seed))
    spreads = {'L0_cond_b3': (0.0, 0.1), 'L0_cond_b2': (0.0, 0.763)}
    factors = {}
    for name, (base, spread) in spreads.items():
        noise = np.random.default_rng([zlib.crc32(name.encode()), seed]).standard_normal(out[name].shape)
        drawn = base * np.exp(spread * noise) if base else spread * noise
        out[name] = jnp.asarray(drawn.astype(out[name].dtype))
    for name, factor in factors.items():
        out[name] = (out[name] * factor).astype(out[name].dtype)
    return out
```

```python
import concourse.bass as bass
from concourse import mybir
from contextlib import ExitStack

F32 = mybir.dt.float32
F32R = mybir.dt.float32r
I32 = mybir.dt.int32
ALU = mybir.AluOpType
ACT = mybir.ActivationFunctionType
AX = mybir.AxisListType.X

P = 128
TOPK = 6
CAP = 64
EXP_UNDERFLOW = -87.3365447
TAKEN = 5.0
SENTINEL = 1.0


def adaln_moe_ffn_kernel(nc, x, cond, W3, b3, W2, b2, gate_w, w_gate, w_up, w_down,
                         sw_gate, sw_up, sw_down, out):
    B, N, D = x.shape
    T = B * N
    Q = cond.shape[1]
    E, _, I = w_gate.shape
    IS = sw_gate.shape[1]
    CH = 512
    NCH = T // CH
    J = CH // P
    KC = D // P
    QC = Q // P
    BPT = P // N
    BPC = CH // N
    NT = IS // P
    TAIL = IS - NT * P
    KT = NT + 1
    GT = 2 * NT + 1
    ROW = D + E
    IT = -(-I // P)
    ITAIL = I - (IT - 1) * P
    NP = E // 2
    NR = CAP // 8
    assert P == 2 * CAP and N == CAP and TAIL == P // 2 and B == P and NP * 2 == E and E == 64

    xf = x.rearrange("b n d -> (b n) d")
    of = out
    table = nc.dram_tensor("table", [T + CAP, ROW], F32, kind="Internal").ap()

    ctx = ExitStack()
    with ctx:
        arena_bytes = 207 * 1024 + 512
        arena = ctx.enter_context(nc.sbuf_tensor("arena", [P, arena_bytes // 4], F32))
        base = nc.sbuf_base - arena_bytes

        class Place:

            def __init__(self, at):
                self.at = at

            def __call__(self, name, shape, dt=F32):
                n = 4
                for s in shape[1:]:
                    n *= s
                t = nc.alloc_sbuf_tensor_at(name, shape, dt, offset=self.at)
                self.at += -(-n // 32) * 32
                assert self.at <= base + arena_bytes, (name, self.at - base)
                return t

        def sem(name):
            return ctx.enter_context(nc.semaphore(name))

        fore = Place(base)
        w2h = fore("w2h", [P, KC, D], F32R)
        w2l = fore("w2l", [P, KC, D], F32R)
        guh = fore("guh", [P, KC, 2 * IS], F32R)
        gul = fore("gul", [P, KC, 2 * IS], F32R)
        xh = fore("xh", [P, 2, D], F32R)
        xl = fore("xl", [P, 2, D], F32R)
        xm = fore("xm", [P, 2, CH])
        xmh = fore("xmh", [P, KC, CH], F32R)
        xml = fore("xml", [P, KC, CH], F32R)

        aft = Place(base)
        wg = [aft(f"wg{s}", [P, 2, KC * I]) for s in range(2)]
        wu = [aft(f"wu{s}", [P, 2, KC * I]) for s in range(2)]
        wd = [aft(f"wd{s}", [P, 2, IT, D]) for s in range(2)]
        hg = [aft(f"hg{s}", [P, ROW]) for s in range(2)]
        hgt = [aft(f"hgt{s}", [P, KC, P]) for s in range(2)]
        esilu = [aft(f"esilu{s}", [P, IT, CAP]) for s in range(2)]
        eact = [aft(f"eact{s}", [P, IT, CAP]) for s in range(2)]
        ysc = [aft(f"ysc{s}", [P, D]) for s in range(2)]
        assert aft.at <= fore.at, (aft.at - base, fore.at - base)

        keep = Place(fore.at)
        sdh = keep("sdh", [P, KT, D], F32R)
        sdl = keep("sdl", [P, KT, D], F32R)
        gwh = keep("gwh", [P, KC, E], F32R)
        gwl = keep("gwl", [P, KC, E], F32R)
        hh = keep("hh", [P, KC, CH], F32R)
        hl = keep("hl", [P, KC, CH], F32R)
        h32 = keep("h32", [P, 2, CH])
        prod = keep("prod", [P, 2, CH])
        outst = keep("outst", [P, 2, D])
        hrow = keep("hrow", [P, J, ROW])
        qT = keep("qT", [P, KC, B])
        ident = keep("ident", [P, P])
        mixr = keep("mixr", [P, P], F32R)
        b2c = keep("b2c", [P, KC])
        b3c = keep("b3c", [P, KC])
        tokrank = keep("tokrank", [P, T // P])
        top = keep("top", [P, J, 8])
        pick = keep("pick", [P, J, 8])
        z = keep("z", [P, J, E])
        zx = keep("zx", [P, J, E + 2])
        marked = keep("marked", [P, J, E + 2])
        ez_at = keep.at
        ez = keep("ez", [P, J, E])
        ranks = keep("ranks", [P, J, E])
        ssum = keep("ssum", [P, J])
        rsum = keep("rsum", [P, J])
        cand = keep("cand", [E, CAP + CH])
        first = keep("first", [E, CAP])
        slot_no = keep("slot_no", [NP, P])
        firstp = keep("firstp", [NP, P])
        slotp = keep("slotp", [NP, P])
        idx_pair = keep("idx_pair", [P, NP], I32)
        idx_hi = keep("idx_hi", [CAP, NP], I32)
        gidx = [keep(f"gidx{s}", [P, 1], I32) for s in range(2)]
        sidx = [keep(f"sidx{s}", [CAP, 1], I32) for s in range(2)]
        x_at = keep.at
        x32 = keep("x32", [P, 2 * J * D])
        a_at = keep.at
        ah = keep("ah", [P, KT, CH], F32R)
        al = keep("al", [P, KT, CH], F32R)

        st = Place(a_at)
        stage = [st(f"stage{s}", [P, 4 * D]) for s in range(3)]
        assert st.at <= keep.at
        cs = Place(x_at + J * D * 4)
        w3s = cs("w3s", [P, QC, D])
        conds = cs("conds", [B, Q])
        condT = cs("condT", [P, QC, B])
        assert cs.at <= a_at
        gws = cs("gws", [E, D])
        assert cs.at <= a_at
        mix32 = Place(ez_at)("mix32", [P, P])
        zrows = hrow[0:CAP, 0, :]

        bank = [ctx.enter_context(nc.psum_tensor(f"bank{i}", [P, 512], F32)) for i in range(8)]

        class Sems:
            cond_loaded = sem("cond_loaded")
            bias_loaded = sem("bias_loaded")
            gate_loaded = sem("gate_loaded")
            x_loaded = sem("x_loaded")
            zero_rows = sem("zero_rows")
            pads_stored = sem("pads_stored")
            consts_ident = sem("consts_ident")
            slotno_ready = sem("slotno_ready")
            presets = sem("presets")
            mix32_ready = sem("mix32_ready")
            mixr_ready = sem("mixr_ready")
            condT_filled = sem("condT_filled")
            condT_ready = sem("condT_ready")
            q_filled = sem("q_filled")
            q_ready = sem("q_ready")
            gateT_filled = sem("gateT_filled")
            gwh_ready = sem("gwh_ready")
            gwl_ready = sem("gwl_ready")
            stage_split_h = sem("stage_split_h")
            stage_split_l = sem("stage_split_l")
            xh_ready = sem("xh_ready")
            xl_ready = sem("xl_ready")
            xt_filled = sem("xt_filled")
            xm_ready = sem("xm_ready")
            xmh_ready = sem("xmh_ready")
            xml_ready = sem("xml_ready")
            cond_filled = sem("cond_filled")
            cond_taken = sem("cond_taken")
            hh_ready = sem("hh_ready")
            hl_ready = sem("hl_ready")
            rows_filled = sem("rows_filled")
            rows_taken = sem("rows_taken")
            logits_filled = sem("logits_filled")
            route_step = sem("route_step")
            z_ready = sem("z_ready")
            exp_ready = sem("exp_ready")
            ranks_ready = sem("ranks_ready")
            scores_ready = sem("scores_ready")
            table_stored = sem("table_stored")
            ranksT_filled = sem("ranksT_filled")
            merge_step = sem("merge_step")
            gu_filled = sem("gu_filled")
            silu_ready = sem("silu_ready")
            prod_ready = sem("prod_ready")
            ah_ready = sem("ah_ready")
            al_ready = sem("al_ready")
            down_filled = sem("down_filled")
            down_taken = sem("down_taken")
            rank_step = sem("rank_step")
            slots_filled = sem("slots_filled")
            slots_ready = sem("slots_ready")
            idx_copied = sem("idx_copied")
            rowsT_filled = sem("rowsT_filled")
            rowsT_ready = sem("rowsT_ready")
            egate_filled = sem("egate_filled")
            esilu_ready = sem("esilu_ready")
            eact_ready = sem("eact_ready")
            edown_filled = sem("edown_filled")
            y_ready = sem("y_ready")
            scattered = sem("scattered")
            passed = sem("passed")

        stage_loaded = [sem(f"stage_loaded{s}") for s in range(3)]
        out_stored = [sem(f"out_stored{s}") for s in range(2)]
        gathered = [sem(f"gathered{s}") for s in range(2)]
        wgu_loaded = [sem(f"wgu_loaded{s}") for s in range(2)]
        wd_loaded = [sem(f"wd_loaded{s}") for s in range(2)]
        s = Sems

        def wait(eng, semaphore, value):
            if isinstance(value, int) and value <= 0:
                return
            eng.wait_ge(semaphore, value)

        def of_slot(each, p, q):
            return each // 2 * p + each - each // 2 * q

        def wait_apart(eng, semaphore, value):
            if isinstance(value, int):
                wait(eng, semaphore, value)
            else:
                eng.wait_ge(semaphore, value)
                eng.sem_inc(s.passed, 1)

        w2v = W2.rearrange("(kc p) o -> p kc o", p=P)
        sgv = sw_gate.rearrange("(kc p) i -> p kc i", p=P)
        suv = sw_up.rearrange("(kc p) i -> p kc i", p=P)
        sdv = sw_down[0:NT * P, :].rearrange("(k p) o -> p k o", p=P)

        def stage_view(n, k, w):
            return stage[n % 3][:, 0:k * w].rearrange("p (k w) -> p k w", k=k)

        pieces = [([(w2v, stage_view(0, KC, D))], [(w2h[:, :, :], w2l[:, :, :], stage_view(0, KC, D))])]
        for src, at in ((sgv, 0), (suv, 1)):
            for k0 in (0, 2):
                v = stage_view(len(pieces), 2, IS)
                main = slice(at * NT * P, (at + 1) * NT * P)
                tail = slice(2 * NT * P + at * TAIL, 2 * NT * P + (at + 1) * TAIL)
                pieces.append(([(src[:, k0:k0 + 2, :], v)],
                               [(guh[:, k0:k0 + 2, main], gul[:, k0:k0 + 2, main], v[:, :, 0:NT * P]),
                                (guh[:, k0:k0 + 2, tail], gul[:, k0:k0 + 2, tail], v[:, :, NT * P:IS])]))
        v = stage_view(len(pieces), 3, D)
        pieces.append(([(sdv[:, 0:3, :], v)], [(sdh[:, 0:3, :], sdl[:, 0:3, :], v)]))
        v = stage_view(len(pieces), 3, D)
        pieces.append(([(sdv[:, 3:NT, :], v[:, 0:NT - 3, :]), (sw_down[NT * P:IS, :], v[0:TAIL, NT - 3, :])],
                       [(sdh[:, 3:NT, :], sdl[:, 3:NT, :], v[:, 0:NT - 3, :]),
                        (sdh[0:TAIL, NT, :], sdl[0:TAIL, NT, :], v[0:TAIL, NT - 3, :])]))
        splits_before = [sum(len(p[1]) for p in pieces[:n]) for n in range(len(pieces) + 1)]
        loads_before = [sum(len(p[0]) for q, p in enumerate(pieces[:n]) if q % 3 == (n - 1) % 3)
                        for n in range(1, len(pieces) + 1)]
        W2_SPLIT, GU_SPLIT, SD_SPLIT = splits_before[1], splits_before[5], splits_before[7]

        def x_tile(n, j):
            return x32[:, bass.ds((n % 2) * (J * D) + j * D, D)]

        def x_chunk(n):
            return x32[:, bass.ds((n % 2) * (J * D), J * D)]

        def xm_tile(t, j):
            return t[:, :, j * P:(j + 1) * P]

        block = ctx.enter_context(nc.Block())

        @block.sync
        def _(sp):
            def load_x(n):
                wait(sp, s.down_taken, J * (n - 1))
                sp.dma_start(x_chunk(n).rearrange("p (j d) -> p j d", j=J),
                             xf[bass.ds(n * CH, CH), :].rearrange("(j p) d -> p j d", p=P)).then_inc(s.x_loaded, 16)

            def store_rows(n):
                sp.wait_ge(s.q_ready, 1)
                sp.wait_ge(s.scores_ready, n + 1)
                sp.wait_ge(s.rows_taken, KC * (n + 1))
                sp.dma_start(table[bass.ds(n * CH, CH), :].rearrange("(j p) r -> p j r", p=P),
                             hrow[:, :, :]).then_inc(s.table_stored, 16)

            def store_out(c, j):
                sp.wait_ge(s.down_taken, J * c + j + 1)
                sp.dma_start(of[bass.ds(c * CH + j * P, P), :], outst[:, j % 2, :]).then_inc(out_stored[j % 2], 16)

            def chunk(c, last):
                if not last:
                    load_x(c + 1)
                store_rows(c)
                for j in range(J):
                    store_out(c, j)

            sp.dma_start(conds[:, :], cond).then_inc(s.cond_loaded, 16)
            sp.dma_start(w3s[:, :, :], W3.rearrange("(k p) o -> p k o", p=P)).then_inc(s.cond_loaded, 16)
            sp.dma_start(x32[:, 0:J * D].rearrange("p (j d) -> p j d", j=J),
                         xf[0:CH, :].rearrange("(j p) d -> p j d", p=P)).then_inc(s.x_loaded, 16)
            with nc.allow_non_contiguous_dma(reason="two vectors of 512 elements, once"):
                sp.dma_start(b3c[:, :], b3.rearrange("(k p) -> p k", p=P)).then_inc(s.bias_loaded, 16)
                sp.dma_start(b2c[:, :], b2.rearrange("(k p) -> p k", p=P)).then_inc(s.bias_loaded, 16)
            sp.dma_start(gws[:, :], gate_w).then_inc(s.gate_loaded, 16)
            sp.wait_ge(s.zero_rows, 1)
            sp.dma_start(table[T:T + CAP, :], zrows).then_inc(s.pads_stored, 16)
            sp.dma_start(of[T:T + CAP, :], zrows[:, 0:D]).then_inc(s.pads_stored, 16)
            for n, (loads, _) in enumerate(pieces):
                if n >= 3:
                    sp.wait_ge(s.stage_split_l, splits_before[n - 2])
                for src, dst in loads:
                    sp.dma_start(dst, src).then_inc(stage_loaded[n % 3], 16)
            sp.wait_ge(s.q_ready, 1)
            sp.wait_ge(s.gateT_filled, 1)
            sp.wait_ge(s.mixr_ready, 1)
            chunk(0, False)
            with sp.Fori(1, NCH - 1) as c:
                chunk(c, False)
            chunk(NCH - 1, True)

            def pairs(w, how, **kw):
                return w.rearrange(how, two=2, **kw)
            gv = pairs(w_gate, "(two e) (p kc) n -> e p two (kc n)", kc=KC)
            uv = pairs(w_up, "(two e) (p kc) n -> e p two (kc n)", kc=KC)
            dv = w_down.rearrange("(two e) i d -> e i two d", two=2)

            def load_pair(p, q, first_pair):
                wait(sp, s.egate_filled, 2 * (p - 1) if not first_pair else 0)
                sp.dma_start(wg[q][:, :, :], gv[bass.ds(p, 1)].rearrange("o p two n -> (o p) two n")).then_inc(wgu_loaded[q], 16)
                sp.dma_start(wu[q][:, :, :], uv[bass.ds(p, 1)].rearrange("o p two n -> (o p) two n")).then_inc(wgu_loaded[q], 16)
                wait(sp, s.edown_filled, 2 * (p - 1) if not first_pair else 0)
                for it in range(IT):
                    m = ITAIL if it == IT - 1 else P
                    sp.dma_start(wd[q][0:m, :, it, :],
                                 dv[bass.ds(p, 1), it * P:it * P + m].rearrange("o p two n -> (o p) two n")).then_inc(wd_loaded[q], 16)

            sp.wait_ge(s.gu_filled, GT * NCH)
            load_pair(0, 0, True)
            load_pair(1, 1, True)
            with sp.Fori(1, NP // 2) as i:
                for q in range(2):
                    load_pair(2 * i + q, q, False)
            for q in range(2):
                sp.wait_ge(out_stored[q], 32 * NCH)
            sp.wait_ge(s.table_stored, 16 * NCH)
            sp.wait_ge(s.pads_stored, 32)
            sp.wait_ge(s.scattered, 32 * NP)

        @block.gpsimd
        def _(pool):
            nc.gpsimd.memset(ident[:, :], 0.0).then_inc(s.consts_ident, 1)
            pool.wait_ge(s.consts_ident, 1)
            nc.gpsimd.affine_select(out=ident[:, :], in_=ident[:, :], compare_op=ALU.not_equal, fill=1.0, base=0,
                                    pattern=[[-1, P]], channel_multiplier=1).then_inc(s.consts_ident, 1)
            nc.gpsimd.iota(tokrank[:, :], pattern=[[-P, T // P]], base=T, channel_multiplier=-1,
                           allow_small_or_imprecise_dtypes=True).then_inc(s.slotno_ready, 1)
            nc.gpsimd.iota(slot_no[:, :], pattern=[[0, 2], [1, CAP]], base=0, channel_multiplier=0,
                           allow_small_or_imprecise_dtypes=True).then_inc(s.slotno_ready, 1)

            def gather(p, q):
                nc.gpsimd.tensor_copy(gidx[q][:, :], idx_pair[:, bass.ds(p, 1)])
                nc.gpsimd.tensor_copy(sidx[q][:, :], idx_hi[:, bass.ds(p, 1)]).then_inc(s.idx_copied, 1)
                wait(pool, s.y_ready, p - 1)
                wait_apart(pool, s.idx_copied, p + 1)
                nc.gpsimd.indirect_dma_start(
                    out=hg[q][:, :], out_offset=None, in_=table,
                    in_offset=bass.IndirectOffsetOnAxis(ap=gidx[q][:, :], axis=0)).then_inc(gathered[q], 16)

            def scatter(p, q):
                for e, idx in ((0, gidx[q][0:CAP, :]), (1, sidx[q][:, :])):
                    if e == 0:
                        pool.wait_ge(s.y_ready, p + 1)
                    wait_apart(pool, s.scattered, 32 * p + 16 * e)
                    nc.gpsimd.indirect_dma_start(
                        out=of, out_offset=bass.IndirectOffsetOnAxis(ap=idx, axis=0),
                        in_=ysc[q][e * CAP:(e + 1) * CAP, :], in_offset=None,
                        compute_op=ALU.add).then_inc(s.scattered, 16)

            pool.wait_ge(s.slots_ready, 1)
            pool.wait_ge(s.table_stored, 16 * NCH)
            pool.wait_ge(s.pads_stored, 32)
            pool.wait_ge(s.down_taken, J * NCH)
            for q in range(2):
                pool.wait_ge(out_stored[q], 32 * NCH)
            gather(0, 0)
            gather(1, 1)
            scatter(0, 0)
            with pool.Fori(0, NP // 2 - 1) as i:
                for q in range(2):
                    p = 2 * i + 1 + q
                    pool.wait_ge(s.scattered, 32 * p)
                    gather(p + 1, q)
                    scatter(p, 1 - q)
            scatter(NP - 1, 1)
            pool.wait_ge(s.scattered, 32 * NP)

        @block.scalar
        def _(act):
            def copy(o, i):
                return nc.scalar.activation(o, i, ACT.Copy)

            def split_x(n, j):
                if j == 0:
                    act.wait_ge(s.x_loaded, 16 * (n + 1))
                wait(act, s.xt_filled, J * n + j - 1)
                copy(xh[:, j % 2, :], x_tile(n, j)).then_inc(s.xh_ready, 1)

            def split_xm(n, j):
                if j == 0:
                    wait(act, s.cond_filled, KC * n)
                act.wait_ge(s.xm_ready, J * n + j + 1)
                copy(xm_tile(xmh, j), xm[:, j % 2, :].rearrange("p (k t) -> p k t", k=KC)).then_inc(s.xmh_ready, 1)

            def take_cond(n, oc):
                act.wait_ge(s.cond_filled, KC * n + oc + 1)
                if oc >= 2:
                    act.wait_ge(s.rows_filled, KC * n + oc - 1)
                    act.wait_ge(s.hl_ready, KC * n + oc - 1)
                else:
                    wait(act, s.rows_filled, KC * n)
                    wait(act, s.hl_ready, KC * n)
                if oc == 0:
                    wait(act, s.gu_filled, GT * n)
                nc.scalar.activation(h32[:, oc % 2, :], bank[5 + oc % 2][:, :], ACT.Relu,
                                     bias=b2c[:, oc:oc + 1]).then_inc(s.cond_taken, 1)
                act.wait_ge(s.cond_taken, KC * n + oc + 1)
                copy(hh[:, oc, :], h32[:, oc % 2, :]).then_inc(s.hh_ready, 1)

            def take_rows(n, oc):
                if oc == 0:
                    wait(act, s.table_stored, 16 * n)
                act.wait_ge(s.rows_filled, KC * n + oc + 1)
                copy(hrow[:, :, oc * P:(oc + 1) * P],
                     bank[2 * (oc % 2)][:, :].rearrange("p (j f) -> p j f", j=J)).then_inc(s.rows_taken, 1)

            def exp_scores(c):
                act.wait_ge(s.z_ready, c + 1)
                nc.scalar.activation(ez[:, :, :], z[:, :, :], ACT.Exp).then_inc(s.exp_ready, 1)

            def silu(c, i):
                t = min(2 * i, GT - 1)
                act.wait_ge(s.gu_filled, GT * c + t + 1)
                wait(act, s.al_ready, KT * c + max(i - 1, 0))
                m = TAIL if i == NT else P
                nc.scalar.activation(prod[0:m, i % 2, :], bank[t % 3][0:m, :], ACT.Silu).then_inc(s.silu_ready, 1)

            def split_a(c, i):
                if i == 0:
                    wait(act, s.down_filled, J * c)
                act.wait_ge(s.prod_ready, KT * c + i + 1)
                m = TAIL if i == NT else P
                copy(ah[0:m, i, :], prod[0:m, i % 2, :]).then_inc(s.ah_ready, 1)

            def chunk(c, last):
                n = c + 1
                silu(c, 0)
                if not last:
                    split_x(n, 0)
                    split_x(n, 1)
                exp_scores(c)
                silu(c, 1)
                split_a(c, 0)
                silu(c, 2)
                split_a(c, 1)
                if not last:
                    split_x(n, 2)
                    split_x(n, 3)
                    split_xm(n, 0)
                    split_xm(n, 1)
                silu(c, 3)
                split_a(c, 2)
                if not last:
                    split_xm(n, 2)
                    split_xm(n, 3)
                silu(c, 4)
                split_a(c, 3)
                silu(c, 5)
                split_a(c, 4)
                split_a(c, 5)
                if not last:
                    adaln(n)

            def adaln(n):
                take_cond(n, 0)
                take_cond(n, 1)
                take_rows(n, 0)
                take_cond(n, 2)
                take_rows(n, 1)
                take_cond(n, 3)
                take_rows(n, 2)
                take_rows(n, 3)

            act.wait_ge(s.mix32_ready, 1)
            copy(mixr[:, :], mix32[:, :]).then_inc(s.mixr_ready, 1)
            split_x(0, 0)
            split_x(0, 1)
            act.wait_ge(s.condT_filled, 1)
            copy(condT[:, :, :], bank[5][:, 0:QC * B].rearrange("p (k b) -> p k b", k=QC)).then_inc(s.condT_ready, 1)
            act.wait_ge(s.bias_loaded, 32)
            act.wait_ge(s.q_filled, 1)
            for fc in range(KC):
                last = nc.scalar.activation(qT[:, fc, :], bank[6][:, fc * B:(fc + 1) * B], ACT.Relu,
                                            bias=b3c[:, fc:fc + 1])
            last.then_inc(s.q_ready, 1)

            def split_piece(n):
                act.wait_ge(stage_loaded[n % 3], 16 * loads_before[n])
                for h_part, _, src in pieces[n][1]:
                    copy(h_part, src).then_inc(s.stage_split_h, 1)

            split_piece(0)
            for j in range(J):
                if j + 2 < J:
                    split_x(0, j + 2)
                split_xm(0, j)
            act.wait_ge(s.gateT_filled, 1)
            copy(gwh[:, :, :], bank[7][:, 0:KC * E].rearrange("p (k e) -> p k e", k=KC)).then_inc(s.gwh_ready, 1)
            split_piece(1)
            split_piece(2)
            split_piece(3)
            split_piece(4)
            act.wait_ge(s.pads_stored, 32)
            adaln(0)
            split_piece(5)
            split_piece(6)
            chunk(0, False)
            with act.Fori(1, NCH - 1) as c:
                chunk(c, False)
            chunk(NCH - 1, True)

            def take_rowsT(p, q):
                act.wait_ge(s.rowsT_filled, p + 1)
                wait(act, s.egate_filled, 2 * (p - 1))
                copy(hgt[q][:, :, :], bank[6 + q][:, :].rearrange("p (k t) -> p k t", k=KC)).then_inc(s.rowsT_ready, 1)

            def esilu_pair(p, q):
                for e in range(2):
                    act.wait_ge(s.egate_filled, 2 * p + e + 1)
                    wait(act, s.eact_ready, 2 * p)
                    g = bank[2 * e]
                    nc.scalar.activation(esilu[e][:, 0:IT - 1, :],
                                         g[:, 0:(IT - 1) * CAP].rearrange("p (i t) -> p i t", t=CAP), ACT.Silu)
                    nc.scalar.activation(esilu[e][0:ITAIL, IT - 1, :], g[0:ITAIL, (IT - 1) * CAP:IT * CAP],
                                         ACT.Silu).then_inc(s.esilu_ready, 1)

            take_rowsT(0, 0)
            esilu_pair(0, 0)
            take_rowsT(1, 1)
            esilu_pair(1, 1)
            with act.Fori(1, NP // 2) as i:
                for q in range(2):
                    p = 2 * i + q
                    take_rowsT(p, q)
                    esilu_pair(p, q)

        @block.vector
        def _(dve):
            def lower(o, full, high):
                return nc.vector.tensor_tensor(o, full, high.bitcast(F32), ALU.subtract)

            def split_x(n, j):
                dve.wait_ge(s.xh_ready, J * n + j + 1)
                lower(xl[:, j % 2, :], x_tile(n, j), xh[:, j % 2, :]).then_inc(s.xl_ready, 1)

            def take_xt(n, j):
                dve.wait_ge(s.xt_filled, J * n + j + 1)
                if j >= 2:
                    dve.wait_ge(s.xml_ready, J * n + j - 1)
                else:
                    wait(dve, s.xml_ready, J * n)
                nc.vector.tensor_tensor(
                    xm[:, j % 2, :].rearrange("p (k b t) -> p k b t", k=KC, b=BPT),
                    bank[3 + j % 2][:, :].rearrange("p (k b t) -> p k b t", k=KC, b=BPT),
                    qT[:, :, bass.ds(n * BPC + j * BPT, BPT)].unsqueeze(3).to_broadcast([P, KC, BPT, N]),
                    ALU.mult).then_inc(s.xm_ready, 1)

            def split_xm(n, j):
                dve.wait_ge(s.xmh_ready, J * n + j + 1)
                lower(xm_tile(xml, j), xm[:, j % 2, :].rearrange("p (k t) -> p k t", k=KC),
                      xm_tile(xmh, j)).then_inc(s.xml_ready, 1)

            def split_h(n, oc):
                dve.wait_ge(s.hh_ready, KC * n + oc + 1)
                lower(hl[:, oc, :], h32[:, oc % 2, :], hh[:, oc, :]).then_inc(s.hl_ready, 1)

            def product(c, i):
                t = min(2 * i + 1, GT - 1)
                dve.wait_ge(s.gu_filled, GT * c + t + 1)
                dve.wait_ge(s.silu_ready, KT * c + i + 1)
                m, up0 = (TAIL, TAIL) if i == NT else (P, 0)
                nc.vector.tensor_tensor(prod[0:m, i % 2, :], bank[t % 3][up0:up0 + m, :], prod[0:m, i % 2, :],
                                        ALU.mult).then_inc(s.prod_ready, 1)

            def split_a(c, i):
                dve.wait_ge(s.ah_ready, KT * c + i + 1)
                m = TAIL if i == NT else P
                lower(al[0:m, i, :], prod[0:m, i % 2, :], ah[0:m, i, :]).then_inc(s.al_ready, 1)

            def take_down(c, j):
                dve.wait_ge(s.down_filled, J * c + j + 1)
                wait(dve, out_stored[j % 2], 16 * (2 * c + j // 2))
                nc.vector.tensor_tensor(outst[:, j % 2, :], bank[3 + j % 2][:, :], x_tile(c, j),
                                        ALU.add).then_inc(s.down_taken, 1)

            ROUTE_STEPS = 6

            def route(c):
                lg = bank[7][:, 0:J * E].rearrange("p (j e) -> p j e", j=J)
                step = [ROUTE_STEPS * c]

                def link(op):
                    step[0] = step[0] + 1
                    op.then_inc(s.route_step, 1)
                    dve.wait_ge(s.route_step, step[0])

                wait_apart(dve, s.logits_filled, c + 1)
                for j in range(J):
                    op = nc.vector.max(top[:, j, :], lg[:, j, :])
                link(op)
                nc.vector.tensor_tensor(pick[:, :, 0:TOPK], top[:, :, 0:TOPK],
                                        top[:, :, 0:1].to_broadcast([P, J, TOPK]), ALU.subtract)
                link(nc.vector.tensor_tensor(z[:, :, :], lg, top[:, :, 0:1].to_broadcast([P, J, E]), ALU.subtract))
                nc.vector.tensor_scalar(zx[:, :, 0:E], z[:, :, :], EXP_UNDERFLOW, None, ALU.max).then_inc(s.z_ready, 1)
                nc.vector.tensor_scalar(pick[:, :, 0:TOPK], pick[:, :, 0:TOPK], EXP_UNDERFLOW, None,
                                        ALU.max).then_inc(s.route_step, 1)
                step[0] = step[0] + 1
                wait_apart(dve, s.route_step, step[0])
                for j in range(J):
                    op = nc.vector.match_replace(marked[:, j, :], pick[:, j, :], zx[:, j, :], TAKEN)
                link(op)
                for j in range(J):
                    op = nc.vector.tensor_scalar(ranks[:, j, :], marked[:, j, 0:E], TAKEN - 1.0,
                                                 tokrank[:, bass.ds(c * J + j, 1)], ALU.is_ge, ALU.mult)
                op.then_inc(s.ranks_ready, 1)
                dve.wait_ge(s.exp_ready, c + 1)
                link(nc.vector.reduce_sum(ssum[:, :], ez[:, :, :], AX))
                link(nc.vector.reciprocal(rsum[:, :], ssum[:, :]))
                wait(dve, s.table_stored, 16 * c)
                nc.vector.tensor_tensor(hrow[:, :, D:ROW], ez[:, :, :],
                                        rsum[:, :].unsqueeze(2).to_broadcast([P, J, E]),
                                        ALU.mult).then_inc(s.scores_ready, 1)

            MERGE_STEPS = 1 + 2 * NR

            def take_ranksT(c):
                dve.wait_ge(s.ranksT_filled, c + 1)
                nc.vector.tensor_copy(cand[:, CAP:CAP + CH], bank[7][0:E, :]).then_inc(s.merge_step, 1)

            def merge(c, r):
                eight = first[:, 8 * r:8 * r + 8]
                wait_apart(dve, s.merge_step, MERGE_STEPS * c + 1 + 2 * r)
                nc.vector.max(eight, cand[:, :]).then_inc(s.merge_step, 1)
                wait_apart(dve, s.merge_step, MERGE_STEPS * c + 2 + 2 * r)
                if r < NR - 1:
                    nc.vector.match_replace(cand[:, :], eight, cand[:, :], 0.0).then_inc(s.merge_step, 1)
                else:
                    nc.vector.tensor_copy(cand[:, 0:CAP], first[:, :]).then_inc(s.merge_step, 1)

            def chunk(c, last):
                n = c + 1
                route(c)
                product(c, 0)
                if not last:
                    split_x(n, 0)
                    split_x(n, 1)
                product(c, 1)
                split_a(c, 0)
                product(c, 2)
                split_a(c, 1)
                if not last:
                    split_x(n, 2)
                    split_x(n, 3)
                    take_xt(n, 0)
                    take_xt(n, 1)
                    split_xm(n, 0)
                    split_xm(n, 1)
                product(c, 3)
                split_a(c, 2)
                if not last:
                    take_xt(n, 2)
                    take_xt(n, 3)
                    split_xm(n, 2)
                    split_xm(n, 3)
                product(c, 4)
                split_a(c, 3)
                product(c, 5)
                split_a(c, 4)
                split_a(c, 5)
                take_ranksT(c)
                for r in range(KC):
                    merge(c, r)
                    if not last:
                        split_h(n, r)
                for j in range(J):
                    take_down(c, j)
                    merge(c, KC + j)

            nc.vector.memset(hrow[0:CAP, 0, :], 0.0).then_inc(s.zero_rows, 1)
            nc.vector.memset(cand[:, 0:CAP], 0.0).then_inc(s.presets, 1)
            nc.vector.memset(pick[:, :, TOPK:8], SENTINEL).then_inc(s.presets, 1)
            nc.vector.memset(zx[:, :, E:E + 2], SENTINEL).then_inc(s.presets, 1)
            nc.vector.memset(mix32[:, :], 0.0).then_inc(s.presets, 1)
            dve.wait_ge(s.presets, 4)
            for b in range(BPT):
                nc.vector.memset(mix32[b * N:(b + 1) * N, b * N:(b + 1) * N], 1.0).then_inc(s.presets, 1)
            dve.wait_ge(s.presets, 4 + BPT)
            dve.wait_ge(s.consts_ident, 2)
            nc.vector.scalar_tensor_tensor(out=mix32[:, :], in0=ident[:, :], scalar=float(N), in1=mix32[:, :],
                                           op0=ALU.mult, op1=ALU.add).then_inc(s.mix32_ready, 1)
            dve.wait_ge(s.slotno_ready, 2)
            split_x(0, 0)
            split_x(0, 1)

            def split_piece(n):
                for k, (_, l_part, src) in enumerate(pieces[n][1]):
                    dve.wait_ge(s.stage_split_h, splits_before[n] + k + 1)
                    high = pieces[n][1][k][0]
                    lower(l_part, src, high).then_inc(s.stage_split_l, 1)

            split_piece(0)
            dve.wait_ge(s.q_ready, 1)
            for j in range(J):
                if j + 2 < J:
                    take_xt(0, j)
                    split_x(0, j + 2)
                else:
                    take_xt(0, j)
                split_xm(0, j)
            dve.wait_ge(s.gwh_ready, 1)
            lower(gwl[:, :, :], bank[7][:, 0:KC * E].rearrange("p (k e) -> p k e", k=KC),
                  gwh[:, :, :]).then_inc(s.gwl_ready, 1)
            split_piece(1)
            split_piece(2)
            split_piece(3)
            split_piece(4)
            for oc in range(KC):
                split_h(0, oc)
            split_piece(5)
            split_piece(6)
            dve.wait_ge(s.pads_stored, 32)
            chunk(0, False)
            with dve.Fori(1, NCH - 1) as c:
                chunk(c, False)
            chunk(NCH - 1, True)

            done = [0]

            def link(op):
                done[0] += 1
                op.then_inc(s.rank_step, 1)
                dve.wait_ge(s.rank_step, done[0])

            for half in range(2):
                op = nc.vector.tensor_copy(firstp[:, half * CAP:(half + 1) * CAP], first[half * NP:(half + 1) * NP, :])
            link(op)
            link(nc.vector.scalar_tensor_tensor(out=slotp[:, :], in0=firstp[:, :], scalar=0.0, in1=slot_no[:, :],
                                                op0=ALU.is_equal, op1=ALU.mult))
            link(nc.vector.tensor_tensor(slotp[:, :], slotp[:, :], firstp[:, :], ALU.subtract))
            dve.wait_ge(s.slots_filled, 1)
            nc.vector.tensor_scalar(idx_pair[:, :], bank[5][:, 0:NP], float(T), None, ALU.add)
            nc.vector.tensor_scalar(idx_hi[:, :], bank[5][0:CAP, NP:2 * NP], float(T), None,
                                    ALU.add).then_inc(s.slots_ready, 1)

            def eproduct(p, q):
                for e in range(2):
                    dve.wait_ge(s.esilu_ready, 2 * p + e + 1)
                    wait(dve, s.edown_filled, 2 * p + e - 1)
                    u = bank[2 * e + 1]
                    nc.vector.tensor_tensor(eact[e][:, 0:IT - 1, :],
                                            u[:, 0:(IT - 1) * CAP].rearrange("p (i t) -> p i t", t=CAP),
                                            esilu[e][:, 0:IT - 1, :], ALU.mult)
                    nc.vector.tensor_tensor(eact[e][0:ITAIL, IT - 1, :], u[0:ITAIL, (IT - 1) * CAP:IT * CAP],
                                            esilu[e][0:ITAIL, IT - 1, :], ALU.mult).then_inc(s.eact_ready, 1)

            def scale_y(p, q):
                dve.wait_ge(s.edown_filled, 2 * (p + 1))
                wait(dve, s.scattered, 32 * (p - 1))
                for e in range(2):
                    rows = slice(e * CAP, (e + 1) * CAP)
                    op = nc.vector.tensor_scalar(ysc[q][rows, :], bank[4 + q][rows, :],
                                                 hg[q][rows, bass.ds(p + D + e * NP, 1)], None, ALU.mult)
                op.then_inc(s.y_ready, 1)

            eproduct(0, 0)
            scale_y(0, 0)
            eproduct(1, 1)
            scale_y(1, 1)
            with dve.Fori(1, NP // 2) as i:
                for q in range(2):
                    p = 2 * i + q
                    eproduct(p, q)
                    scale_y(p, q)

        @block.tensor
        def _(pe):
            def three(o, st_h, st_l, mv_h, mv_l, first_mm, last_mm):
                nc.tensor.matmul(o, st_h, mv_h, start=first_mm, stop=False)
                nc.tensor.matmul(o, st_h, mv_l, start=False, stop=False)
                return nc.tensor.matmul(o, st_l, mv_h, start=False, stop=last_mm)

            def mix_x(n, j):
                pe.wait_ge(s.xh_ready, J * n + j + 1)
                pe.wait_ge(s.xl_ready, J * n + j + 1)
                if j < 2:
                    wait(pe, s.down_taken, J * (n - 1))
                else:
                    pe.wait_ge(s.xm_ready, J * n + j - 1)
                for k in range(KC):
                    o = bank[3 + j % 2][:, k * P:(k + 1) * P]
                    nc.tensor.matmul(o, xh[:, j % 2, k * P:(k + 1) * P], mixr[:, :], start=True, stop=False)
                    op = nc.tensor.matmul(o, xl[:, j % 2, k * P:(k + 1) * P], mixr[:, :], start=False, stop=True)
                op.then_inc(s.xt_filled, 1)

            def cond_tile(n, oc):
                if oc == 0:
                    pe.wait_ge(s.xmh_ready, J * (n + 1))
                    pe.wait_ge(s.xml_ready, J * (n + 1))
                if oc >= 2:
                    pe.wait_ge(s.cond_taken, KC * n + oc - 1)
                else:
                    wait(pe, s.cond_taken, KC * n)
                for k in range(KC):
                    cols = slice(oc * P, (oc + 1) * P)
                    op = three(bank[5 + oc % 2][:, :], w2h[:, k, cols], w2l[:, k, cols], xmh[:, k, :], xml[:, k, :],
                               k == 0, k == KC - 1)
                op.then_inc(s.cond_filled, 1)

            def rows_tile(n, oc):
                pe.wait_ge(s.cond_taken, KC * n + oc + 1)
                if oc >= 2:
                    pe.wait_ge(s.rows_taken, KC * n + oc - 1)
                elif oc == 0:
                    wait(pe, s.prod_ready, KT * n)
                for j in range(J):
                    op = nc.tensor.transpose(bank[2 * (oc % 2)][:, j * P:(j + 1) * P],
                                             h32[:, oc % 2, j * P:(j + 1) * P], ident[:, :])
                op.then_inc(s.rows_filled, 1)

            def logits(n):
                pe.wait_ge(s.hh_ready, KC * (n + 1))
                pe.wait_ge(s.hl_ready, KC * (n + 1))
                wait(pe, s.merge_step, (2 * NR + 1) * (n - 1) + 1 if not (isinstance(n, int) and n == 0) else 0)
                for j in range(J):
                    for k in range(KC):
                        t = slice(j * P, (j + 1) * P)
                        op = three(bank[7][:, j * E:(j + 1) * E], hh[:, k, t], hl[:, k, t], gwh[:, k, :], gwl[:, k, :],
                                   k == 0, k == KC - 1)
                op.then_inc(s.logits_filled, 1)

            def gu_tile(c, t):
                if t == 0:
                    pe.wait_ge(s.hl_ready, KC * (c + 1))
                    pe.wait_ge(s.rows_taken, KC * (c + 1))
                    pe.wait_ge(s.prod_ready, KT * c) if not isinstance(c, int) or c else None
                if t >= 3:
                    u = t - 3
                    if u % 2 == 0:
                        pe.wait_ge(s.silu_ready, KT * c + u // 2 + 1)
                    else:
                        pe.wait_ge(s.prod_ready, KT * c + u // 2 + 1)
                i = t // 2
                cols = slice(2 * NT * P, 2 * IS) if t == GT - 1 else slice((t % 2) * NT * P + i * P, (t % 2) * NT * P + (i + 1) * P)
                for k in range(KC):
                    op = three(bank[t % 3][:, :], guh[:, k, cols], gul[:, k, cols], hh[:, k, :], hl[:, k, :],
                               k == 0, k == KC - 1)
                op.then_inc(s.gu_filled, 1)

            def ranksT(c):
                wait_apart(pe, s.ranks_ready, c + 1)
                for j in range(J):
                    op = nc.tensor.transpose(bank[7][0:E, j * P:(j + 1) * P], ranks[:, j, :], ident[:, :])
                op.then_inc(s.ranksT_filled, 1)

            def down_tile(c, j, last):
                if j == 0:
                    pe.wait_ge(s.ah_ready, KT * (c + 1))
                    pe.wait_ge(s.al_ready, KT * (c + 1))
                if j < 2:
                    pe.wait_ge(s.xm_ready, J * (c + 1) if last else J * (c + 2))
                    if last:
                        pe.wait_ge(s.down_taken, J * c)
                else:
                    pe.wait_ge(s.down_taken, J * c + j - 1)
                for k in range(KT):
                    m = TAIL if k == NT else P
                    t = slice(j * P, (j + 1) * P)
                    op = three(bank[3 + j % 2][:, :], ah[0:m, k, t], al[0:m, k, t], sdh[0:m, k, :], sdl[0:m, k, :],
                               k == 0, k == KT - 1)
                op.then_inc(s.down_filled, 1)

            def chunk(c, last):
                n = c + 1
                for t in range(GT):
                    gu_tile(c, t)
                    if not last and t == 5:
                        mix_x(n, 0)
                        mix_x(n, 1)
                    if not last and t == 7:
                        mix_x(n, 2)
                        mix_x(n, 3)
                ranksT(c)
                if not last:
                    adaln_head(n)
                down_tile(c, 0, last)
                if not last:
                    rows_tile(n, 3)
                down_tile(c, 1, last)
                if not last:
                    logits(n)
                down_tile(c, 2, last)
                down_tile(c, 3, last)

            def adaln_head(n):
                cond_tile(n, 0)
                cond_tile(n, 1)
                rows_tile(n, 0)
                cond_tile(n, 2)
                rows_tile(n, 1)
                cond_tile(n, 3)
                rows_tile(n, 2)

            pe.wait_ge(s.consts_ident, 2)
            pe.wait_ge(s.cond_loaded, 32)
            for k in range(QC):
                op = nc.tensor.transpose(bank[5][:, k * B:(k + 1) * B], conds[:, k * P:(k + 1) * P], ident[:, :])
            op.then_inc(s.condT_filled, 1)
            pe.wait_ge(s.condT_ready, 1)
            for fc in range(KC):
                for k in range(QC):
                    op = nc.tensor.matmul(bank[6][:, fc * B:(fc + 1) * B], w3s[:, k, fc * P:(fc + 1) * P],
                                          condT[:, k, :], start=(k == 0), stop=(k == QC - 1))
            op.then_inc(s.q_filled, 1)
            pe.wait_ge(s.gate_loaded, 16)
            for k in range(KC):
                op = nc.tensor.transpose(bank[7][:, k * E:(k + 1) * E], gws[:, k * P:(k + 1) * P], ident[0:E, 0:E])
            op.then_inc(s.gateT_filled, 1)
            pe.wait_ge(s.mixr_ready, 1)
            for j in range(J):
                mix_x(0, j)
            pe.wait_ge(s.q_ready, 1)
            pe.wait_ge(s.stage_split_l, W2_SPLIT)
            adaln_head(0)
            rows_tile(0, 3)
            pe.wait_ge(s.gwl_ready, 1)
            logits(0)
            pe.wait_ge(s.stage_split_l, SD_SPLIT)
            chunk(0, False)
            with pe.Fori(1, NCH - 1) as c:
                chunk(c, False)
            chunk(NCH - 1, True)

            pe.wait_ge(s.rank_step, 3)
            nc.tensor.transpose(bank[5][:, 0:NP], slotp[:, :], ident[0:NP, 0:NP])
            nc.tensor.transpose(bank[5][0:CAP, NP:2 * NP], slotp[:, CAP:P], ident[0:NP, 0:NP]).then_inc(s.slots_filled, 1)

            def rowsT(p, q):
                pe.wait_ge(gathered[q], of_slot(16, p, q))
                wait(pe, s.rowsT_ready, p - 1)
                v = hg[q][:, 0:D].rearrange("t (p k) -> t k p", k=KC)
                for k in range(KC):
                    op = nc.tensor.transpose(bank[6 + q][:, k * P:(k + 1) * P], v[:, k, :], ident[:, :])
                op.then_inc(s.rowsT_filled, 1)

            def egate(p, q, e):
                if e == 0:
                    pe.wait_ge(s.rowsT_ready, p + 1)
                    pe.wait_ge(wgu_loaded[q], of_slot(32, p, q))
                wait(pe, s.eact_ready, 2 * p)
                for w, b in ((wg[q], bank[2 * e]), (wu[q], bank[2 * e + 1])):
                    for it in range(IT):
                        m = ITAIL if it == IT - 1 else P
                        for k in range(KC):
                            op = nc.tensor.matmul(b[0:m, it * CAP:(it + 1) * CAP],
                                                  w[:, e, k * I + it * P:k * I + it * P + m],
                                                  hgt[q][:, k, e * CAP:(e + 1) * CAP],
                                                  start=(k == 0), stop=(k == KC - 1))
                op.then_inc(s.egate_filled, 1)

            def edown(p, q, e):
                pe.wait_ge(s.eact_ready, 2 * p + e + 1)
                if e == 0:
                    pe.wait_ge(wd_loaded[q], of_slot(16 * IT, p, q))
                    wait(pe, s.y_ready, p - 1)
                for it in range(IT):
                    m = ITAIL if it == IT - 1 else P
                    op = nc.tensor.matmul(bank[4 + q][e * CAP:(e + 1) * CAP, :], eact[e][0:m, it, :],
                                          wd[q][0:m, e, it, :], start=(it == 0), stop=(it == IT - 1))
                op.then_inc(s.edown_filled, 1)

            def pair(p, q, last):
                egate(p, q, 0)
                egate(p, q, 1)
                edown(p, q, 0)
                if not last:
                    rowsT(p + 1, 1 - q)
                edown(p, q, 1)

            rowsT(0, 0)
            pair(0, 0, False)
            pair(1, 1, False)
            with pe.Fori(1, NP // 2 - 1) as i:
                for q in range(2):
                    pair(2 * i + q, q, False)
            pair(NP - 2, 0, False)
            pair(NP - 1, 1, True)


_INS = ['x', 'cond_1024', 'L0_cond_W3', 'L0_cond_b3', 'L0_cond_W2', 'L0_cond_b2', 'L0_ffn_gate_w',
        'L0_ffn_w_gate', 'L0_ffn_w_up', 'L0_ffn_w_down', 'L0_ffn_sw_gate', 'L0_ffn_sw_up', 'L0_ffn_sw_down']


def kernel(**inputs):
    import numpy as _np
    import concourse.bacc as _bacc
    from concourse import mybir as _mybir
    from concourse.bass_utils import run_bass_kernel_spmd as _run

    nc = _bacc.Bacc("TRN2", target_bir_lowering=False, num_devices=1)
    arrays, args = {}, []
    for name in _INS:
        a = _np.ascontiguousarray(inputs[name])
        arrays[f"in_{name}_dram"] = a
        args.append(nc.dram_tensor(f"in_{name}_dram", a.shape, _mybir.dt.from_np(a.dtype), kind="ExternalInput").ap())
    b, n, d = inputs['x'].shape
    args.append(nc.dram_tensor("out_0_dram", (b * n + CAP, d), _mybir.dt.float32, kind="ExternalOutput").ap())
    adaln_moe_ffn_kernel(nc, *args)
    r = _run(nc, [arrays], core_ids=[0])
    return r.results[0]["out_0_dram"][:b * n].reshape(b, n, d)
```

```python
import concourse.bass as bass
from concourse import mybir
from contextlib import ExitStack

F32 = mybir.dt.float32
F32R = mybir.dt.float32r
I32 = mybir.dt.int32
ALU = mybir.AluOpType
ACT = mybir.ActivationFunctionType
AX = mybir.AxisListType.X

P = 128
TOPK = 6
CAP = 64
EXP_UNDERFLOW = -87.3365447
TAKEN = 5.0
SENTINEL = 1.0


def adaln_moe_ffn_kernel(nc, x, cond, W3, b3, W2, b2, gate_w, w_gate, w_up, w_down,
                         sw_gate, sw_up, sw_down, out):
    B, N, D = x.shape
    T = B * N
    Q = cond.shape[1]
    E, _, I = w_gate.shape
    IS = sw_gate.shape[1]
    CH = 512
    NCH = T // CH
    J = CH // P
    KC = D // P
    QC = Q // P
    BPT = P // N
    BPC = CH // N
    NT = IS // P
    TAIL = IS - NT * P
    KT = NT + 1
    GT = 2 * NT + 1
    ROW = D + E
    IT = -(-I // P)
    ITAIL = I - (IT - 1) * P
    NP = E // 2
    NR = CAP // 8
    assert P == 2 * CAP and N == CAP and TAIL == P // 2 and B == P and NP * 2 == E and E == 64

    xf = x.rearrange("b n d -> (b n) d")
    of = out
    table = nc.dram_tensor("table", [T + CAP, ROW], F32, kind="Internal").ap()

    ctx = ExitStack()
    with ctx:
        arena_bytes = 207 * 1024 + 512
        arena = ctx.enter_context(nc.sbuf_tensor("arena", [P, arena_bytes // 4], F32))
        base = nc.sbuf_base - arena_bytes

        class Place:

            def __init__(self, at):
                self.at = at

            def __call__(self, name, shape, dt=F32):
                n = 4
                for s in shape[1:]:
                    n *= s
                t = nc.alloc_sbuf_tensor_at(name, shape, dt, offset=self.at)
                self.at += -(-n // 32) * 32
                assert self.at <= base + arena_bytes, (name, self.at - base)
                return t

        def sem(name):
            return ctx.enter_context(nc.semaphore(name))

        fore = Place(base)
        w2h = fore("w2h", [P, KC, D], F32R)
        w2l = fore("w2l", [P, KC, D], F32R)
        guh = fore("guh", [P, KC, 2 * IS], F32R)
        gul = fore("gul", [P, KC, 2 * IS], F32R)
        xs = fore("xs", [P, 2, D])
        xm = fore("xm", [P, 2, CH])
        xmh = fore("xmh", [P, KC, CH], F32R)
        xml = fore("xml", [P, KC, CH], F32R)

        aft = Place(base)
        wg = [aft(f"wg{s}", [P, 2, KC * I]) for s in range(2)]
        wu = [aft(f"wu{s}", [P, 2, KC * I]) for s in range(2)]
        wd = [aft(f"wd{s}", [P, 2, IT, D]) for s in range(2)]
        esilu = [aft(f"esilu{s}", [P, IT, CAP]) for s in range(2)]
        eact = [aft(f"eact{s}", [P, IT, CAP]) for s in range(2)]
        ysc = [aft(f"ysc{s}", [P, D]) for s in range(2)]
        assert aft.at <= fore.at, (aft.at - base, fore.at - base)

        keep = Place(fore.at)
        sdh = keep("sdh", [P, KT, D], F32R)
        sdl = keep("sdl", [P, KT, D], F32R)
        gw2 = keep("gw2", [P, KC, 2 * E], F32R)
        lsb = keep("lsb", [P, CH])
        fold = keep("fold", [P, E])
        vsum = keep("vsum", [P, 2, KC, BPT])
        hh_at = keep.at
        hh = keep("hh", [P, KC, CH], F32R)
        hl = keep("hl", [P, KC, CH], F32R)
        hl_end = keep.at
        h32 = keep("h32", [P, 2, CH])
        prod = keep("prod", [P, 2, CH])
        outst = keep("outst", [P, 2, D])
        hrow = keep("hrow", [P, J, ROW])
        qT = keep("qT", [P, KC, B])
        ident = keep("ident", [P, P])
        qnT = keep("qnT", [P, KC, B])
        b2c = keep("b2c", [P, KC])
        b3c = keep("b3c", [P, KC])
        tokrank = keep("tokrank", [P, T // P])
        top = keep("top", [P, J, 8])
        pick = keep("pick", [P, J, 8])
        z = keep("z", [P, J, E])
        zx = keep("zx", [P, J, E + 2])
        marked = keep("marked", [P, J, E + 2])
        ez = keep("ez", [P, J, E])
        ranks = keep("ranks", [P, J, E])
        ssum = keep("ssum", [P, J])
        rsum = keep("rsum", [P, J])
        cand = keep("cand", [E, CAP + CH])
        first = keep("first", [E, CAP])
        slot_no = keep("slot_no", [NP, P])
        firstp = keep("firstp", [NP, P])
        slotp = keep("slotp", [NP, P])
        idx_pair = keep("idx_pair", [P, NP], I32)
        idx_hi = keep("idx_hi", [CAP, NP], I32)
        gidx = [keep(f"gidx{s}", [P, 1], I32) for s in range(4)]
        sidx = [keep(f"sidx{s}", [CAP, 1], I32) for s in range(4)]
        x_at = keep.at
        x32 = keep("x32", [P, 2 * J * D])
        a_at = keep.at
        ah = keep("ah", [P, KT, CH], F32R)
        al = keep("al", [P, NT, CH], F32R)

        rows_at = Place(hh_at)
        hg = [rows_at(f"hg{s}", [P, ROW]) for s in range(4)]
        hgt = [rows_at(f"hgt{s}", [P, KC, P]) for s in range(2)]
        assert rows_at.at <= hl_end

        st = Place(a_at)
        stage = [st(f"stage{s}", [P, 4 * D]) for s in range(3)]
        assert st.at <= base + arena_bytes
        cs = Place(x_at + J * D * 4)
        w3s = cs("w3s", [P, QC, D])
        conds = cs("conds", [B, Q])
        condT = cs("condT", [P, QC, B])
        assert cs.at <= a_at
        gws = cs("gws", [E, D])
        assert cs.at <= a_at
        zrows = hrow[0:CAP, 0, :]

        bank = [ctx.enter_context(nc.psum_tensor(f"bank{i}", [P, 512], F32)) for i in range(8)]

        class Sems:
            cond_loaded = sem("cond_loaded")
            bias_loaded = sem("bias_loaded")
            gate_loaded = sem("gate_loaded")
            x_loaded = sem("x_loaded")
            zero_rows = sem("zero_rows")
            pads_stored = sem("pads_stored")
            consts_ident = sem("consts_ident")
            slotno_ready = sem("slotno_ready")
            presets = sem("presets")
            condT_filled = sem("condT_filled")
            condT_ready = sem("condT_ready")
            q_filled = sem("q_filled")
            q_ready = sem("q_ready")
            gateT_filled = sem("gateT_filled")
            stage_split_h = sem("stage_split_h")
            stage_split_l = sem("stage_split_l")
            xs_ready = sem("xs_ready")
            gw2_ready = sem("gw2_ready")
            fold_ready = sem("fold_ready")
            vsum_step = sem("vsum_step")
            xt_filled = sem("xt_filled")
            xm_ready = sem("xm_ready")
            xmh_ready = sem("xmh_ready")
            xml_ready = sem("xml_ready")
            cond_filled = sem("cond_filled")
            cond_taken = sem("cond_taken")
            hh_ready = sem("hh_ready")
            hl_ready = sem("hl_ready")
            rows_filled = sem("rows_filled")
            rows_taken = sem("rows_taken")
            lraw_filled = sem("lraw_filled")
            lraw_taken = sem("lraw_taken")
            logits_filled = sem("logits_filled")
            route_step = sem("route_step")
            z_ready = sem("z_ready")
            exp_ready = sem("exp_ready")
            ranks_ready = sem("ranks_ready")
            scores_ready = sem("scores_ready")
            table_stored = sem("table_stored")
            ranksT_filled = sem("ranksT_filled")
            merge_step = sem("merge_step")
            gu_filled = sem("gu_filled")
            silu_ready = sem("silu_ready")
            prod_ready = sem("prod_ready")
            ah_ready = sem("ah_ready")
            al_ready = sem("al_ready")
            down_filled = sem("down_filled")
            down_taken = sem("down_taken")
            rank_step = sem("rank_step")
            slots_filled = sem("slots_filled")
            slots_ready = sem("slots_ready")
            idx_copied = sem("idx_copied")
            rowsT_filled = sem("rowsT_filled")
            rowsT_ready = sem("rowsT_ready")
            egate_filled = sem("egate_filled")
            esilu_ready = sem("esilu_ready")
            eact_ready = sem("eact_ready")
            edown_filled = sem("edown_filled")
            y_ready = sem("y_ready")
            scattered = sem("scattered")
            passed = sem("passed")

        stage_loaded = [sem(f"stage_loaded{s}") for s in range(3)]
        out_stored = [sem(f"out_stored{s}") for s in range(2)]
        gathered = [sem(f"gathered{s}") for s in range(4)]
        wgu_loaded = [sem(f"wgu_loaded{s}") for s in range(2)]
        wd_loaded = [sem(f"wd_loaded{s}") for s in range(2)]
        s = Sems

        def wait(eng, semaphore, value):
            if isinstance(value, int) and value <= 0:
                return
            eng.wait_ge(semaphore, value)

        def of_slot(each, ring, p, q):
            return each // ring * p + each - each // ring * q

        def wait_apart(eng, semaphore, value):
            if isinstance(value, int):
                wait(eng, semaphore, value)
            else:
                eng.wait_ge(semaphore, value)
                eng.sem_inc(s.passed, 1)

        w2v = W2.rearrange("(kc p) o -> p kc o", p=P)
        sgv = sw_gate.rearrange("(kc p) i -> p kc i", p=P)
        suv = sw_up.rearrange("(kc p) i -> p kc i", p=P)
        sdv = sw_down[0:NT * P, :].rearrange("(k p) o -> p k o", p=P)

        def stage_view(n, k, w):
            return stage[n % 3][:, 0:k * w].rearrange("p (k w) -> p k w", k=k)

        pieces = [([(w2v, stage_view(0, KC, D))], [(w2h[:, :, :], w2l[:, :, :], stage_view(0, KC, D))])]
        for src, at in ((sgv, 0), (suv, 1)):
            for k0 in (0, 2):
                v = stage_view(len(pieces), 2, IS)
                main = slice(at * NT * P, (at + 1) * NT * P)
                tail = slice(2 * NT * P + at * TAIL, 2 * NT * P + (at + 1) * TAIL)
                pieces.append(([(src[:, k0:k0 + 2, :], v)],
                               [(guh[:, k0:k0 + 2, main], gul[:, k0:k0 + 2, main], v[:, :, 0:NT * P]),
                                (guh[:, k0:k0 + 2, tail], gul[:, k0:k0 + 2, tail], v[:, :, NT * P:IS])]))
        v = stage_view(len(pieces), 3, D)
        pieces.append(([(sdv[:, 0:3, :], v)], [(sdh[:, 0:3, :], sdl[:, 0:3, :], v)]))
        v = stage_view(len(pieces), 3, D)
        pieces.append(([(sdv[:, 3:NT, :], v[:, 0:NT - 3, :]), (sw_down[NT * P:IS, :], v[0:TAIL, NT - 3, :]),
                        (sw_down[NT * P:IS, :], v[TAIL:P, NT - 3, :])],
                       [(sdh[:, 3:NT + 1, :], sdl[:, 3:NT + 1, :], v)]))
        splits_before = [sum(len(p[1]) for p in pieces[:n]) for n in range(len(pieces) + 1)]
        loads_before = [sum(len(p[0]) for q, p in enumerate(pieces[:n]) if q % 3 == (n - 1) % 3)
                        for n in range(1, len(pieces) + 1)]
        W2_SPLIT, GU_SPLIT, SD_SPLIT = splits_before[1], splits_before[5], splits_before[7]

        def x_tile(n, j):
            return x32[:, bass.ds((n % 2) * (J * D) + j * D, D)]

        def x_chunk(n):
            return x32[:, bass.ds((n % 2) * (J * D), J * D)]

        def xm_tile(t, j):
            return t[:, :, j * P:(j + 1) * P]

        block = ctx.enter_context(nc.Block())

        @block.sync
        def _(sp):
            def load_x(n):
                wait(sp, s.down_taken, J * (n - 1))
                sp.dma_start(x_chunk(n).rearrange("p (j d) -> p j d", j=J),
                             xf[bass.ds(n * CH, CH), :].rearrange("(j p) d -> p j d", p=P)).then_inc(s.x_loaded, 16)

            def store_rows(n):
                sp.wait_ge(s.q_ready, 1)
                sp.wait_ge(s.scores_ready, n + 1)
                sp.wait_ge(s.rows_taken, KC * (n + 1))
                sp.dma_start(table[bass.ds(n * CH, CH), :].rearrange("(j p) r -> p j r", p=P),
                             hrow[:, :, :]).then_inc(s.table_stored, 16)

            def store_out(c, j):
                sp.wait_ge(s.down_taken, J * c + j + 1)
                sp.dma_start(of[bass.ds(c * CH + j * P, P), :], outst[:, j % 2, :]).then_inc(out_stored[j % 2], 16)

            def chunk(c, last):
                if not last:
                    load_x(c + 1)
                store_rows(c)
                for j in range(J):
                    store_out(c, j)

            sp.dma_start(conds[:, :], cond).then_inc(s.cond_loaded, 16)
            sp.dma_start(w3s[:, :, :], W3.rearrange("(k p) o -> p k o", p=P)).then_inc(s.cond_loaded, 16)
            sp.dma_start(x32[:, 0:J * D].rearrange("p (j d) -> p j d", j=J),
                         xf[0:CH, :].rearrange("(j p) d -> p j d", p=P)).then_inc(s.x_loaded, 16)
            with nc.allow_non_contiguous_dma(reason="two vectors of 512 elements, once"):
                sp.dma_start(b3c[:, :], b3.rearrange("(k p) -> p k", p=P)).then_inc(s.bias_loaded, 16)
                sp.dma_start(b2c[:, :], b2.rearrange("(k p) -> p k", p=P)).then_inc(s.bias_loaded, 16)
            sp.dma_start(gws[:, :], gate_w).then_inc(s.gate_loaded, 16)
            sp.wait_ge(s.zero_rows, 1)
            sp.dma_start(table[T:T + CAP, :], zrows).then_inc(s.pads_stored, 16)
            sp.dma_start(of[T:T + CAP, :], zrows[:, 0:D]).then_inc(s.pads_stored, 16)
            for n, (loads, _) in enumerate(pieces):
                if n >= 3:
                    sp.wait_ge(s.stage_split_l, splits_before[n - 2])
                for src, dst in loads:
                    sp.dma_start(dst, src).then_inc(stage_loaded[n % 3], 16)
            sp.wait_ge(s.q_ready, 1)
            sp.wait_ge(s.gateT_filled, 1)
            chunk(0, False)
            with sp.Fori(1, NCH - 1) as c:
                chunk(c, False)
            chunk(NCH - 1, True)

            def pairs(w, how, **kw):
                return w.rearrange(how, two=2, **kw)
            gv = pairs(w_gate, "(two e) (p kc) n -> e p two (kc n)", kc=KC)
            uv = pairs(w_up, "(two e) (p kc) n -> e p two (kc n)", kc=KC)
            dv = w_down.rearrange("(two e) i d -> e i two d", two=2)

            def load_pair(p, q, first_pair):
                wait(sp, s.egate_filled, 2 * (p - 1) if not first_pair else 0)
                sp.dma_start(wg[q][:, :, :], gv[bass.ds(p, 1)].rearrange("o p two n -> (o p) two n")).then_inc(wgu_loaded[q], 16)
                sp.dma_start(wu[q][:, :, :], uv[bass.ds(p, 1)].rearrange("o p two n -> (o p) two n")).then_inc(wgu_loaded[q], 16)
                wait(sp, s.edown_filled, 2 * (p - 1) if not first_pair else 0)
                for it in range(IT):
                    m = ITAIL if it == IT - 1 else P
                    sp.dma_start(wd[q][0:m, :, it, :],
                                 dv[bass.ds(p, 1), it * P:it * P + m].rearrange("o p two n -> (o p) two n")).then_inc(wd_loaded[q], 16)

            sp.wait_ge(s.gu_filled, GT * NCH)
            load_pair(0, 0, True)
            load_pair(1, 1, True)
            with sp.Fori(1, NP // 2) as i:
                for q in range(2):
                    load_pair(2 * i + q, q, False)
            for q in range(2):
                sp.wait_ge(out_stored[q], 32 * NCH)
            sp.wait_ge(s.table_stored, 16 * NCH)
            sp.wait_ge(s.pads_stored, 32)
            sp.wait_ge(s.scattered, 32 * NP)

        @block.gpsimd
        def _(pool):
            nc.gpsimd.memset(ident[:, :], 0.0).then_inc(s.consts_ident, 1)
            pool.wait_ge(s.consts_ident, 1)
            nc.gpsimd.affine_select(out=ident[:, :], in_=ident[:, :], compare_op=ALU.not_equal, fill=1.0, base=0,
                                    pattern=[[-1, P]], channel_multiplier=1).then_inc(s.consts_ident, 1)
            nc.gpsimd.iota(tokrank[:, :], pattern=[[-P, T // P]], base=T, channel_multiplier=-1,
                           allow_small_or_imprecise_dtypes=True).then_inc(s.slotno_ready, 1)
            nc.gpsimd.iota(slot_no[:, :], pattern=[[0, 2], [1, CAP]], base=0, channel_multiplier=0,
                           allow_small_or_imprecise_dtypes=True).then_inc(s.slotno_ready, 1)

            def gather(p, q):
                wait(pool, s.scattered, 32 * (p - 3))
                nc.gpsimd.tensor_copy(gidx[q][:, :], idx_pair[:, bass.ds(p, 1)])
                nc.gpsimd.tensor_copy(sidx[q][:, :], idx_hi[:, bass.ds(p, 1)]).then_inc(s.idx_copied, 1)
                wait(pool, s.y_ready, p - 3)
                wait_apart(pool, s.idx_copied, p + 1)
                nc.gpsimd.indirect_dma_start(
                    out=hg[q][:, :], out_offset=None, in_=table,
                    in_offset=bass.IndirectOffsetOnAxis(ap=gidx[q][:, :], axis=0)).then_inc(gathered[q], 16)

            def scatter(p, q):
                for e, idx in ((0, gidx[q][0:CAP, :]), (1, sidx[q][:, :])):
                    if e == 0:
                        pool.wait_ge(s.y_ready, p + 1)
                    wait_apart(pool, s.scattered, 32 * p + 16 * e)
                    nc.gpsimd.indirect_dma_start(
                        out=of, out_offset=bass.IndirectOffsetOnAxis(ap=idx, axis=0),
                        in_=ysc[q % 2][e * CAP:(e + 1) * CAP, :], in_offset=None,
                        compute_op=ALU.add).then_inc(s.scattered, 16)

            pool.wait_ge(s.slots_ready, 1)
            pool.wait_ge(s.table_stored, 16 * NCH)
            pool.wait_ge(s.pads_stored, 32)
            pool.wait_ge(s.down_taken, J * NCH)
            for q in range(2):
                pool.wait_ge(out_stored[q], 32 * NCH)
            gather(0, 0)
            gather(1, 1)
            for p in range(4):
                gather(p + 2, (p + 2) % 4)
                scatter(p, p)
            with pool.Fori(1, NP // 4 - 1) as i:
                for q in range(4):
                    gather(4 * i + q + 2, (q + 2) % 4)
                    scatter(4 * i + q, q)
            for p in range(NP - 4, NP):
                if p + 2 < NP:
                    gather(p + 2, (p + 2) % 4)
                scatter(p, p % 4)
            pool.wait_ge(s.scattered, 32 * NP)

        @block.scalar
        def _(act):
            def copy(o, i):
                return nc.scalar.activation(o, i, ACT.Copy)

            def copy_x(n, j):
                if j == 0:
                    act.wait_ge(s.x_loaded, 16 * (n + 1))
                wait(act, s.xt_filled, J * n + j - 1)
                copy(xs[:, j % 2, :], x_tile(n, j)).then_inc(s.xs_ready, 1)

            def split_xm(n, j):
                if j == 0:
                    wait(act, s.cond_filled, KC * n)
                act.wait_ge(s.xm_ready, J * n + j + 1)
                copy(xm_tile(xmh, j), xm[:, j % 2, :].rearrange("p (k t) -> p k t", k=KC)).then_inc(s.xmh_ready, 1)

            def take_cond(n, oc):
                act.wait_ge(s.cond_filled, KC * n + oc + 1)
                if oc >= 2:
                    act.wait_ge(s.rows_filled, KC * n + oc - 1)
                    act.wait_ge(s.hl_ready, KC * n + oc - 1)
                else:
                    wait(act, s.rows_filled, KC * n)
                    wait(act, s.hl_ready, KC * n)
                if oc == 0:
                    wait(act, s.gu_filled, GT * n)
                nc.scalar.activation(h32[:, oc % 2, :], bank[5 + oc % 2][:, :], ACT.Relu,
                                     bias=b2c[:, oc:oc + 1]).then_inc(s.cond_taken, 1)
                act.wait_ge(s.cond_taken, KC * n + oc + 1)
                copy(hh[:, oc, :], h32[:, oc % 2, :]).then_inc(s.hh_ready, 1)

            def take_rows(n, oc):
                if oc == 0:
                    wait(act, s.table_stored, 16 * n)
                act.wait_ge(s.rows_filled, KC * n + oc + 1)
                copy(hrow[:, :, oc * P:(oc + 1) * P],
                     bank[2 * (oc % 2)][:, :].rearrange("p (j f) -> p j f", j=J)).then_inc(s.rows_taken, 1)

            def take_lraw(n):
                act.wait_ge(s.lraw_filled, n + 1)
                wait(act, s.logits_filled, n)
                copy(lsb[:, :], bank[1][:, :]).then_inc(s.lraw_taken, 1)

            def exp_scores(c):
                act.wait_ge(s.z_ready, c + 1)
                nc.scalar.activation(ez[:, :, :], z[:, :, :], ACT.Exp).then_inc(s.exp_ready, 1)

            def silu(c, i):
                t = min(2 * i, GT - 1)
                act.wait_ge(s.gu_filled, GT * c + t + 1)
                wait(act, s.al_ready, KT * c + max(i - 1, 0))
                m = TAIL if i == NT else P
                nc.scalar.activation(prod[0:m, i % 2, :], bank[t % 3][0:m, :], ACT.Silu).then_inc(s.silu_ready, 1)

            def split_a(c, i):
                if i == 0:
                    wait(act, s.down_filled, J * c)
                act.wait_ge(s.prod_ready, KT * c + i + 1)
                m = TAIL if i == NT else P
                copy(ah[0:m, i, :], prod[0:m, i % 2, :]).then_inc(s.ah_ready, 1)

            def chunk(c, last):
                n = c + 1
                silu(c, 0)
                if not last:
                    copy_x(n, 0)
                    copy_x(n, 1)
                exp_scores(c)
                silu(c, 1)
                split_a(c, 0)
                silu(c, 2)
                split_a(c, 1)
                if not last:
                    copy_x(n, 2)
                    copy_x(n, 3)
                    split_xm(n, 0)
                    split_xm(n, 1)
                silu(c, 3)
                split_a(c, 2)
                if not last:
                    split_xm(n, 2)
                    split_xm(n, 3)
                silu(c, 4)
                split_a(c, 3)
                silu(c, 5)
                split_a(c, 4)
                split_a(c, 5)
                if not last:
                    adaln(n)

            def adaln(n):
                take_cond(n, 0)
                take_cond(n, 1)
                take_rows(n, 0)
                take_cond(n, 2)
                take_rows(n, 1)
                take_cond(n, 3)
                take_rows(n, 2)
                take_rows(n, 3)
                take_lraw(n)

            copy_x(0, 0)
            copy_x(0, 1)
            act.wait_ge(s.condT_filled, 1)
            copy(condT[:, :, :], bank[5][:, 0:QC * B].rearrange("p (k b) -> p k b", k=QC)).then_inc(s.condT_ready, 1)
            act.wait_ge(s.bias_loaded, 32)
            act.wait_ge(s.q_filled, 1)
            for fc in range(KC):
                last = nc.scalar.activation(qT[:, fc, :], bank[6][:, fc * B:(fc + 1) * B], ACT.Relu,
                                            bias=b3c[:, fc:fc + 1])
            last.then_inc(s.q_ready, 1)

            def split_piece(n):
                act.wait_ge(stage_loaded[n % 3], 16 * loads_before[n])
                for h_part, _, src in pieces[n][1]:
                    copy(h_part, src).then_inc(s.stage_split_h, 1)

            split_piece(0)
            for j in range(J):
                if j + 2 < J:
                    copy_x(0, j + 2)
                split_xm(0, j)
            act.wait_ge(s.gateT_filled, 1)
            copy(gw2[:, :, 0:E], bank[7][:, 0:KC * E].rearrange("p (k e) -> p k e", k=KC)).then_inc(s.gw2_ready, 1)
            split_piece(1)
            split_piece(2)
            split_piece(3)
            split_piece(4)
            act.wait_ge(s.pads_stored, 32)
            adaln(0)
            split_piece(5)
            split_piece(6)
            chunk(0, False)
            with act.Fori(1, NCH - 1) as c:
                chunk(c, False)
            chunk(NCH - 1, True)

            def take_rowsT(p, q):
                act.wait_ge(s.rowsT_filled, p + 1)
                wait(act, s.egate_filled, 2 * (p - 1))
                copy(hgt[q][:, :, :], bank[6 + q][:, :].rearrange("p (k t) -> p k t", k=KC)).then_inc(s.rowsT_ready, 1)

            def esilu_pair(p, q):
                for e in range(2):
                    act.wait_ge(s.egate_filled, 2 * p + e + 1)
                    wait(act, s.eact_ready, 2 * p)
                    g = bank[2 * e]
                    nc.scalar.activation(esilu[e][:, 0:IT - 1, :],
                                         g[:, 0:(IT - 1) * CAP].rearrange("p (i t) -> p i t", t=CAP), ACT.Silu)
                    nc.scalar.activation(esilu[e][0:ITAIL, IT - 1, :], g[0:ITAIL, (IT - 1) * CAP:IT * CAP],
                                         ACT.Silu).then_inc(s.esilu_ready, 1)

            take_rowsT(0, 0)
            esilu_pair(0, 0)
            take_rowsT(1, 1)
            esilu_pair(1, 1)
            with act.Fori(1, NP // 2) as i:
                for q in range(2):
                    p = 2 * i + q
                    take_rowsT(p, q)
                    esilu_pair(p, q)

        @block.vector
        def _(dve):
            def lower(o, full, high):
                return nc.vector.tensor_tensor(o, full, high.bitcast(F32), ALU.subtract)

            def take_xt(n, j):
                xt = bank[3 + j % 2][:, :].rearrange("p (k b t) -> p k b t", k=KC, b=BPT)
                xm4 = xm[:, j % 2, :].rearrange("p (k b t) -> p k b t", k=KC, b=BPT)
                batches = bass.ds(n * BPC + j * BPT, BPT)
                steps = 3 * (J * n + j)
                wait(dve, s.xm_ready, J * n + j)
                wait(dve, s.xml_ready, J * n + max(j - 1, 0))
                dve.wait_ge(s.xt_filled, J * n + j + 1)
                nc.vector.reduce_sum(vsum[:, 0, :, :], xt, AX).then_inc(s.vsum_step, 1)
                nc.vector.tensor_tensor(xm4, xt, qnT[:, :, batches].unsqueeze(3).to_broadcast([P, KC, BPT, N]),
                                        ALU.mult).then_inc(s.vsum_step, 1)
                dve.wait_ge(s.vsum_step, steps + 2)
                nc.vector.tensor_tensor(vsum[:, 1, :, :], vsum[:, 0, :, :], qT[:, :, batches],
                                        ALU.mult).then_inc(s.vsum_step, 1)
                dve.wait_ge(s.vsum_step, steps + 3)
                nc.vector.tensor_tensor(xm4, xm4, vsum[:, 1, :, :].unsqueeze(3).to_broadcast([P, KC, BPT, N]),
                                        ALU.add).then_inc(s.xm_ready, 1)

            def split_xm(n, j):
                dve.wait_ge(s.xmh_ready, J * n + j + 1)
                lower(xm_tile(xml, j), xm[:, j % 2, :].rearrange("p (k t) -> p k t", k=KC),
                      xm_tile(xmh, j)).then_inc(s.xml_ready, 1)

            def split_h(n, oc):
                dve.wait_ge(s.hh_ready, KC * n + oc + 1)
                lower(hl[:, oc, :], h32[:, oc % 2, :], hh[:, oc, :]).then_inc(s.hl_ready, 1)

            def product(c, i):
                t = min(2 * i + 1, GT - 1)
                dve.wait_ge(s.gu_filled, GT * c + t + 1)
                dve.wait_ge(s.silu_ready, KT * c + i + 1)
                m, up0 = (TAIL, TAIL) if i == NT else (P, 0)
                nc.vector.tensor_tensor(prod[0:m, i % 2, :], bank[t % 3][up0:up0 + m, :], prod[0:m, i % 2, :],
                                        ALU.mult).then_inc(s.prod_ready, 1)

            def split_a(c, i):
                dve.wait_ge(s.ah_ready, KT * c + i + 1)
                if i < NT:
                    lower(al[:, i, :], prod[:, i % 2, :], ah[:, i, :]).then_inc(s.al_ready, 1)
                else:
                    lower(ah[TAIL:P, NT, :], prod[0:TAIL, i % 2, :], ah[0:TAIL, NT, :]).then_inc(s.al_ready, 1)

            def take_down(c, j):
                dve.wait_ge(s.down_filled, J * c + j + 1)
                wait(dve, out_stored[j % 2], 16 * (2 * c + j // 2))
                nc.vector.tensor_tensor(outst[:, j % 2, :], bank[3 + j % 2][:, :], x_tile(c, j),
                                        ALU.add).then_inc(s.down_taken, 1)

            ROUTE_STEPS = 6

            def route(c):
                lg = bank[7][:, 0:J * E].rearrange("p (j e) -> p j e", j=J)
                step = [ROUTE_STEPS * c]

                def link(op):
                    step[0] = step[0] + 1
                    op.then_inc(s.route_step, 1)
                    dve.wait_ge(s.route_step, step[0])

                wait_apart(dve, s.logits_filled, c + 1)
                for j in range(J):
                    op = nc.vector.max(top[:, j, :], lg[:, j, :])
                link(op)
                nc.vector.tensor_tensor(pick[:, :, 0:TOPK], top[:, :, 0:TOPK],
                                        top[:, :, 0:1].to_broadcast([P, J, TOPK]), ALU.subtract)
                link(nc.vector.tensor_tensor(z[:, :, :], lg, top[:, :, 0:1].to_broadcast([P, J, E]), ALU.subtract))
                nc.vector.tensor_scalar(zx[:, :, 0:E], z[:, :, :], EXP_UNDERFLOW, None, ALU.max).then_inc(s.z_ready, 1)
                nc.vector.tensor_scalar(pick[:, :, 0:TOPK], pick[:, :, 0:TOPK], EXP_UNDERFLOW, None,
                                        ALU.max).then_inc(s.route_step, 1)
                step[0] = step[0] + 1
                wait_apart(dve, s.route_step, step[0])
                for j in range(J):
                    op = nc.vector.match_replace(marked[:, j, :], pick[:, j, :], zx[:, j, :], TAKEN)
                link(op)
                for j in range(J):
                    op = nc.vector.tensor_scalar(ranks[:, j, :], marked[:, j, 0:E], TAKEN - 1.0,
                                                 tokrank[:, bass.ds(c * J + j, 1)], ALU.is_ge, ALU.mult)
                op.then_inc(s.ranks_ready, 1)
                product(c, 0)
                dve.wait_ge(s.exp_ready, c + 1)
                link(nc.vector.reduce_sum(ssum[:, :], ez[:, :, :], AX))
                link(nc.vector.reciprocal(rsum[:, :], ssum[:, :]))
                wait(dve, s.table_stored, 16 * c)
                nc.vector.tensor_tensor(hrow[:, :, D:ROW], ez[:, :, :],
                                        rsum[:, :].unsqueeze(2).to_broadcast([P, J, E]),
                                        ALU.mult).then_inc(s.scores_ready, 1)

            MERGE_STEPS = 1 + 2 * NR

            def take_ranksT(c):
                dve.wait_ge(s.ranksT_filled, c + 1)
                nc.vector.tensor_copy(cand[:, CAP:CAP + CH], bank[7][0:E, :]).then_inc(s.merge_step, 1)

            def merge(c, r):
                eight = first[:, 8 * r:8 * r + 8]
                wait_apart(dve, s.merge_step, MERGE_STEPS * c + 1 + 2 * r)
                nc.vector.max(eight, cand[:, :]).then_inc(s.merge_step, 1)
                wait_apart(dve, s.merge_step, MERGE_STEPS * c + 2 + 2 * r)
                if r < NR - 1:
                    nc.vector.match_replace(cand[:, :], eight, cand[:, :], 0.0).then_inc(s.merge_step, 1)
                else:
                    nc.vector.tensor_copy(cand[:, 0:CAP], first[:, :]).then_inc(s.merge_step, 1)

            def chunk(c, last):
                n = c + 1
                route(c)
                product(c, 1)
                split_a(c, 0)
                product(c, 2)
                split_a(c, 1)
                if not last:
                    take_xt(n, 0)
                    take_xt(n, 1)
                    split_xm(n, 0)
                    split_xm(n, 1)
                product(c, 3)
                split_a(c, 2)
                if not last:
                    take_xt(n, 2)
                    take_xt(n, 3)
                    split_xm(n, 2)
                    split_xm(n, 3)
                product(c, 4)
                split_a(c, 3)
                product(c, 5)
                split_a(c, 4)
                split_a(c, 5)
                take_ranksT(c)
                for r in range(KC):
                    merge(c, r)
                    if not last:
                        split_h(n, r)
                for j in range(J):
                    take_down(c, j)
                    merge(c, KC + j)

            nc.vector.memset(hrow[0:CAP, 0, :], 0.0).then_inc(s.zero_rows, 1)
            nc.vector.memset(cand[:, 0:CAP], 0.0).then_inc(s.presets, 1)
            nc.vector.memset(pick[:, :, TOPK:8], SENTINEL).then_inc(s.presets, 1)
            nc.vector.memset(zx[:, :, E:E + 2], SENTINEL).then_inc(s.presets, 1)
            dve.wait_ge(s.presets, 3)
            dve.wait_ge(s.consts_ident, 2)
            nc.vector.tensor_copy(fold[0:E, :], ident[0:E, 0:E]).then_inc(s.fold_ready, 1)
            nc.vector.tensor_copy(fold[E:P, :], ident[E:P, E:P]).then_inc(s.fold_ready, 1)
            dve.wait_ge(s.slotno_ready, 2)

            def split_piece(n):
                for k, (_, l_part, src) in enumerate(pieces[n][1]):
                    dve.wait_ge(s.stage_split_h, splits_before[n] + k + 1)
                    high = pieces[n][1][k][0]
                    lower(l_part, src, high).then_inc(s.stage_split_l, 1)

            split_piece(0)
            dve.wait_ge(s.q_ready, 1)
            nc.vector.tensor_scalar(qnT[:, :, :], qT[:, :, :], float(N), None, ALU.mult).then_inc(s.presets, 1)
            dve.wait_ge(s.presets, 4)
            for j in range(J):
                take_xt(0, j)
                split_xm(0, j)
            dve.wait_ge(s.gw2_ready, 1)
            lower(gw2[:, :, E:2 * E], bank[7][:, 0:KC * E].rearrange("p (k e) -> p k e", k=KC),
                  gw2[:, :, 0:E]).then_inc(s.gw2_ready, 1)
            split_piece(1)
            split_piece(2)
            split_piece(3)
            split_piece(4)
            for oc in range(KC):
                split_h(0, oc)
            split_piece(5)
            split_piece(6)
            dve.wait_ge(s.pads_stored, 32)
            chunk(0, False)
            with dve.Fori(1, NCH - 1) as c:
                chunk(c, False)
            chunk(NCH - 1, True)

            done = [0]

            def link(op):
                done[0] += 1
                op.then_inc(s.rank_step, 1)
                dve.wait_ge(s.rank_step, done[0])

            for half in range(2):
                op = nc.vector.tensor_copy(firstp[:, half * CAP:(half + 1) * CAP], first[half * NP:(half + 1) * NP, :])
            link(op)
            link(nc.vector.scalar_tensor_tensor(out=slotp[:, :], in0=firstp[:, :], scalar=0.0, in1=slot_no[:, :],
                                                op0=ALU.is_equal, op1=ALU.mult))
            link(nc.vector.tensor_tensor(slotp[:, :], slotp[:, :], firstp[:, :], ALU.subtract))
            dve.wait_ge(s.slots_filled, 1)
            nc.vector.tensor_scalar(idx_pair[:, :], bank[5][:, 0:NP], float(T), None, ALU.add)
            nc.vector.tensor_scalar(idx_hi[:, :], bank[5][0:CAP, NP:2 * NP], float(T), None,
                                    ALU.add).then_inc(s.slots_ready, 1)

            def eproduct(p, q):
                for e in range(2):
                    dve.wait_ge(s.esilu_ready, 2 * p + e + 1)
                    wait(dve, s.edown_filled, 2 * p + e - 1)
                    u = bank[2 * e + 1]
                    nc.vector.tensor_tensor(eact[e][:, 0:IT - 1, :],
                                            u[:, 0:(IT - 1) * CAP].rearrange("p (i t) -> p i t", t=CAP),
                                            esilu[e][:, 0:IT - 1, :], ALU.mult)
                    nc.vector.tensor_tensor(eact[e][0:ITAIL, IT - 1, :], u[0:ITAIL, (IT - 1) * CAP:IT * CAP],
                                            esilu[e][0:ITAIL, IT - 1, :], ALU.mult).then_inc(s.eact_ready, 1)

            def scale_y(p, q):
                dve.wait_ge(s.edown_filled, 2 * (p + 1))
                wait(dve, s.scattered, 32 * (p - 1))
                for e in range(2):
                    rows = slice(e * CAP, (e + 1) * CAP)
                    op = nc.vector.tensor_scalar(ysc[q % 2][rows, :], bank[4 + q % 2][rows, :],
                                                 hg[q][rows, bass.ds(p + D + e * NP, 1)], None, ALU.mult)
                op.then_inc(s.y_ready, 1)

            for p in range(4):
                eproduct(p, p)
                scale_y(p, p)
            with dve.Fori(1, NP // 4) as i:
                for q in range(4):
                    eproduct(4 * i + q, q)
                    scale_y(4 * i + q, q)

        @block.tensor
        def _(pe):
            def three(o, st_h, st_l, mv_h, mv_l, first_mm, last_mm):
                nc.tensor.matmul(o, st_h, mv_h, start=first_mm, stop=False)
                nc.tensor.matmul(o, st_h, mv_l, start=False, stop=False)
                return nc.tensor.matmul(o, st_l, mv_h, start=False, stop=last_mm)

            def transpose_x(n, j):
                pe.wait_ge(s.xs_ready, J * n + j + 1)
                if j < 2:
                    wait(pe, s.down_taken, J * (n - 1))
                else:
                    pe.wait_ge(s.xm_ready, J * n + j - 1)
                for k in range(KC):
                    op = nc.tensor.transpose(bank[3 + j % 2][:, k * P:(k + 1) * P],
                                             xs[:, j % 2, k * P:(k + 1) * P], ident[:, :])
                op.then_inc(s.xt_filled, 1)

            def cond_tile(n, oc):
                if oc == 0:
                    pe.wait_ge(s.xmh_ready, J * (n + 1))
                    pe.wait_ge(s.xml_ready, J * (n + 1))
                if oc >= 2:
                    pe.wait_ge(s.cond_taken, KC * n + oc - 1)
                else:
                    wait(pe, s.cond_taken, KC * n)
                for k in range(KC):
                    cols = slice(oc * P, (oc + 1) * P)
                    op = three(bank[5 + oc % 2][:, :], w2h[:, k, cols], w2l[:, k, cols], xmh[:, k, :], xml[:, k, :],
                               k == 0, k == KC - 1)
                op.then_inc(s.cond_filled, 1)

            def rows_tile(n, oc):
                pe.wait_ge(s.cond_taken, KC * n + oc + 1)
                if oc >= 2:
                    pe.wait_ge(s.rows_taken, KC * n + oc - 1)
                elif oc == 0:
                    wait(pe, s.prod_ready, KT * n)
                for j in range(J):
                    op = nc.tensor.transpose(bank[2 * (oc % 2)][:, j * P:(j + 1) * P],
                                             h32[:, oc % 2, j * P:(j + 1) * P], ident[:, :])
                op.then_inc(s.rows_filled, 1)

            def logits_raw(n):
                pe.wait_ge(s.hh_ready, KC * (n + 1))
                pe.wait_ge(s.hl_ready, KC * (n + 1))
                wait(pe, s.prod_ready, KT * n)
                for k in range(KC):
                    if k == KC - 1:
                        nc.tensor.matmul(bank[1][0:E, :], gw2[:, k, 0:E], hl[:, k, :], start=False, stop=False)
                        op = nc.tensor.matmul(bank[1][:, :], gw2[:, k, :], hh[:, k, :], start=False, stop=True)
                    else:
                        nc.tensor.matmul(bank[1][:, :], gw2[:, k, :], hh[:, k, :], start=(k == 0), stop=False)
                        nc.tensor.matmul(bank[1][0:E, :], gw2[:, k, 0:E], hl[:, k, :], start=False, stop=False)
                op.then_inc(s.lraw_filled, 1)

            def logits(n):
                pe.wait_ge(s.lraw_taken, n + 1)
                wait(pe, s.merge_step, (2 * NR + 1) * (n - 1) + 1 if not (isinstance(n, int) and n == 0) else 0)
                for j in range(J):
                    op = nc.tensor.matmul(bank[7][:, j * E:(j + 1) * E], lsb[:, j * P:(j + 1) * P], fold[:, :],
                                          start=True, stop=True)
                op.then_inc(s.logits_filled, 1)

            def gu_tile(c, t):
                if t == 0:
                    pe.wait_ge(s.hl_ready, KC * (c + 1))
                    pe.wait_ge(s.rows_taken, KC * (c + 1))
                    wait(pe, s.prod_ready, KT * c)
                if t == 1:
                    pe.wait_ge(s.lraw_taken, c + 1)
                if t >= 3:
                    u = t - 3
                    if u % 2 == 0:
                        pe.wait_ge(s.silu_ready, KT * c + u // 2 + 1)
                    else:
                        pe.wait_ge(s.prod_ready, KT * c + u // 2 + 1)
                i = t // 2
                cols = slice(2 * NT * P, 2 * IS) if t == GT - 1 else slice((t % 2) * NT * P + i * P, (t % 2) * NT * P + (i + 1) * P)
                for k in range(KC):
                    op = three(bank[t % 3][:, :], guh[:, k, cols], gul[:, k, cols], hh[:, k, :], hl[:, k, :],
                               k == 0, k == KC - 1)
                op.then_inc(s.gu_filled, 1)

            def ranksT(c):
                wait_apart(pe, s.ranks_ready, c + 1)
                for j in range(J):
                    op = nc.tensor.transpose(bank[7][0:E, j * P:(j + 1) * P], ranks[:, j, :], ident[:, :])
                op.then_inc(s.ranksT_filled, 1)

            def down_tile(c, j, last):
                if j == 0:
                    pe.wait_ge(s.ah_ready, KT * (c + 1))
                    pe.wait_ge(s.al_ready, KT * (c + 1))
                if j < 2:
                    pe.wait_ge(s.xm_ready, J * (c + 1) if last else J * (c + 2))
                    if last:
                        pe.wait_ge(s.down_taken, J * c)
                else:
                    pe.wait_ge(s.down_taken, J * c + j - 1)
                o = bank[3 + j % 2][:, :]
                t = slice(j * P, (j + 1) * P)
                for k in range(NT):
                    three(o, ah[:, k, t], al[:, k, t], sdh[:, k, :], sdl[:, k, :], k == 0, False)
                nc.tensor.matmul(o, ah[:, NT, t], sdh[:, NT, :], start=False, stop=False)
                op = nc.tensor.matmul(o, ah[0:TAIL, NT, t], sdl[0:TAIL, NT, :], start=False, stop=True)
                op.then_inc(s.down_filled, 1)

            def chunk(c, last):
                n = c + 1
                for t in range(GT):
                    gu_tile(c, t)
                    if not last and t == 5:
                        transpose_x(n, 0)
                        transpose_x(n, 1)
                    if not last and t == 7:
                        transpose_x(n, 2)
                        transpose_x(n, 3)
                ranksT(c)
                if not last:
                    adaln_head(n)
                down_tile(c, 0, last)
                if not last:
                    rows_tile(n, 3)
                down_tile(c, 1, last)
                if not last:
                    logits_raw(n)
                down_tile(c, 2, last)
                if not last:
                    logits(n)
                down_tile(c, 3, last)

            def adaln_head(n):
                cond_tile(n, 0)
                cond_tile(n, 1)
                rows_tile(n, 0)
                cond_tile(n, 2)
                rows_tile(n, 1)
                cond_tile(n, 3)
                rows_tile(n, 2)

            pe.wait_ge(s.consts_ident, 2)
            pe.wait_ge(s.cond_loaded, 32)
            for k in range(QC):
                op = nc.tensor.transpose(bank[5][:, k * B:(k + 1) * B], conds[:, k * P:(k + 1) * P], ident[:, :])
            op.then_inc(s.condT_filled, 1)
            pe.wait_ge(s.condT_ready, 1)
            for fc in range(KC):
                for k in range(QC):
                    op = nc.tensor.matmul(bank[6][:, fc * B:(fc + 1) * B], w3s[:, k, fc * P:(fc + 1) * P],
                                          condT[:, k, :], start=(k == 0), stop=(k == QC - 1))
            op.then_inc(s.q_filled, 1)
            pe.wait_ge(s.gate_loaded, 16)
            for k in range(KC):
                op = nc.tensor.transpose(bank[7][:, k * E:(k + 1) * E], gws[:, k * P:(k + 1) * P], ident[0:E, 0:E])
            op.then_inc(s.gateT_filled, 1)
            for j in range(J):
                transpose_x(0, j)
            pe.wait_ge(s.q_ready, 1)
            pe.wait_ge(s.stage_split_l, W2_SPLIT)
            adaln_head(0)
            rows_tile(0, 3)
            pe.wait_ge(s.gw2_ready, 2)
            logits_raw(0)
            pe.wait_ge(s.fold_ready, 2)
            logits(0)
            pe.wait_ge(s.stage_split_l, SD_SPLIT)
            chunk(0, False)
            with pe.Fori(1, NCH - 1) as c:
                chunk(c, False)
            chunk(NCH - 1, True)

            pe.wait_ge(s.rank_step, 3)
            nc.tensor.transpose(bank[5][:, 0:NP], slotp[:, :], ident[0:NP, 0:NP])
            nc.tensor.transpose(bank[5][0:CAP, NP:2 * NP], slotp[:, CAP:P], ident[0:NP, 0:NP]).then_inc(s.slots_filled, 1)

            def rowsT(p, q):
                pe.wait_ge(gathered[q], of_slot(16, 4, p, q))
                wait(pe, s.rowsT_ready, p - 1)
                v = hg[q][:, 0:D].rearrange("t (p k) -> t k p", k=KC)
                for k in range(KC):
                    op = nc.tensor.transpose(bank[6 + q % 2][:, k * P:(k + 1) * P], v[:, k, :], ident[:, :])
                op.then_inc(s.rowsT_filled, 1)

            def egate(p, q, e):
                if e == 0:
                    pe.wait_ge(s.rowsT_ready, p + 1)
                    pe.wait_ge(wgu_loaded[q % 2], of_slot(32, 2, p, q % 2))
                wait(pe, s.eact_ready, 2 * p)
                for w, b in ((wg[q % 2], bank[2 * e]), (wu[q % 2], bank[2 * e + 1])):
                    for it in range(IT):
                        m = ITAIL if it == IT - 1 else P
                        for k in range(KC):
                            op = nc.tensor.matmul(b[0:m, it * CAP:(it + 1) * CAP],
                                                  w[:, e, k * I + it * P:k * I + it * P + m],
                                                  hgt[q % 2][:, k, e * CAP:(e + 1) * CAP],
                                                  start=(k == 0), stop=(k == KC - 1))
                op.then_inc(s.egate_filled, 1)

            def edown(p, q, e):
                pe.wait_ge(s.eact_ready, 2 * p + e + 1)
                if e == 0:
                    pe.wait_ge(wd_loaded[q % 2], of_slot(16 * IT, 2, p, q % 2))
                    wait(pe, s.y_ready, p - 1)
                for it in range(IT):
                    m = ITAIL if it == IT - 1 else P
                    op = nc.tensor.matmul(bank[4 + q % 2][e * CAP:(e + 1) * CAP, :], eact[e][0:m, it, :],
                                          wd[q % 2][0:m, e, it, :], start=(it == 0), stop=(it == IT - 1))
                op.then_inc(s.edown_filled, 1)

            def pair(p, q, last):
                egate(p, q, 0)
                egate(p, q, 1)
                edown(p, q, 0)
                if not last:
                    rowsT(p + 1, (q + 1) % 4)
                edown(p, q, 1)

            rowsT(0, 0)
            for p in range(4):
                pair(p, p, False)
            with pe.Fori(1, NP // 4 - 1) as i:
                for q in range(4):
                    pair(4 * i + q, q, False)
            for p in range(NP - 4, NP):
                pair(p, p % 4, p == NP - 1)


_INS = ['x', 'cond_1024', 'L0_cond_W3', 'L0_cond_b3', 'L0_cond_W2', 'L0_cond_b2', 'L0_ffn_gate_w',
        'L0_ffn_w_gate', 'L0_ffn_w_up', 'L0_ffn_w_down', 'L0_ffn_sw_gate', 'L0_ffn_sw_up', 'L0_ffn_sw_down']


def kernel(**inputs):
    import numpy as _np
    import concourse.bacc as _bacc
    from concourse import mybir as _mybir
    from concourse.bass_utils import run_bass_kernel_spmd as _run

    nc = _bacc.Bacc("TRN2", target_bir_lowering=False, num_devices=1)
    arrays, args = {}, []
    for name in _INS:
        a = _np.ascontiguousarray(inputs[name])
        arrays[f"in_{name}_dram"] = a
        args.append(nc.dram_tensor(f"in_{name}_dram", a.shape, _mybir.dt.from_np(a.dtype), kind="ExternalInput").ap())
    b, n, d = inputs['x'].shape
    args.append(nc.dram_tensor("out_0_dram", (b * n + CAP, d), _mybir.dt.float32, kind="ExternalOutput").ap())
    adaln_moe_ffn_kernel(nc, *args)
    r = _run(nc, [arrays], core_ids=[0])
    return r.results[0]["out_0_dram"][:b * n].reshape(b, n, d)
```

```python
import concourse.bass as bass
from concourse import mybir
from contextlib import ExitStack

F32 = mybir.dt.float32
F32R = mybir.dt.float32r
I32 = mybir.dt.int32
ALU = mybir.AluOpType
ACT = mybir.ActivationFunctionType
AX = mybir.AxisListType.X

P = 128
TOPK = 6
CAP = 64
EXP_UNDERFLOW = -87.3365447
TAKEN = 5.0
SENTINEL = 1.0


def adaln_moe_ffn_kernel(nc, x, cond, W3, b3, W2, b2, gate_w, w_gate, w_up, w_down,
                         sw_gate, sw_up, sw_down, out):
    B, N, D = x.shape
    T = B * N
    Q = cond.shape[1]
    E, _, I = w_gate.shape
    IS = sw_gate.shape[1]
    CH = 512
    NCH = T // CH
    J = CH // P
    KC = D // P
    QC = Q // P
    BPT = P // N
    BPC = CH // N
    NT = IS // P
    TAIL = IS - NT * P
    KT = NT + 1
    GT = 2 * NT + 1
    ROW = D + E
    IT = -(-I // P)
    ITAIL = I - (IT - 1) * P
    NP = E // 2
    NR = CAP // 8
    assert P == 2 * CAP and N == CAP and TAIL == P // 2 and B == P and NP * 2 == E and E == 64

    xf = x.rearrange("b n d -> (b n) d")
    of = out
    table = nc.dram_tensor("table", [T + CAP, ROW], F32, kind="Internal").ap()

    ctx = ExitStack()
    with ctx:
        arena_bytes = 207 * 1024 + 512
        arena = ctx.enter_context(nc.sbuf_tensor("arena", [P, arena_bytes // 4], F32))
        base = nc.sbuf_base - arena_bytes

        class Place:

            def __init__(self, at):
                self.at = at

            def __call__(self, name, shape, dt=F32):
                n = 4
                for s in shape[1:]:
                    n *= s
                t = nc.alloc_sbuf_tensor_at(name, shape, dt, offset=self.at)
                self.at += -(-n // 32) * 32
                assert self.at <= base + arena_bytes, (name, self.at - base)
                return t

        def sem(name):
            return ctx.enter_context(nc.semaphore(name))

        fore = Place(base)
        w2h = fore("w2h", [P, KC, D], F32R)
        w2l = fore("w2l", [P, KC, D], F32R)
        xs = fore("xs", [P, 2, D])
        xm = fore("xm", [P, 2, CH])
        xmh = fore("xmh", [P, KC, CH], F32R)
        xml = fore("xml", [P, KC, CH], F32R)
        gu_at = fore.at
        gu = fore("gu", [P, GT, 2, KC, P], F32R)

        def gate_up_at(place, name):
            return [place(f"{name}_{e}", [P, KC * I]) for e in range(2)]

        def down_at(place, name):
            return [place(f"{name}_{e}", [P, IT, D]) for e in range(2)]

        even = Place(base)
        wg = [gate_up_at(even, "wg0")]
        wu = [gate_up_at(even, "wu0")]
        wd = [down_at(even, "wd0")]
        hg = [even(f"hg{r}", [P, ROW]) for r in range(2)]
        eact = [even(f"eact{e}", [P, IT, CAP]) for e in range(2)]
        assert even.at <= gu_at
        GU_STEP = 3
        odd = [Place(gu_at + step * GU_STEP * 2 * KC * P * 4) for step in range(4)]
        wg.append(gate_up_at(odd[0], "wg1"))
        wu.append(gate_up_at(odd[1], "wu1"))
        wd.append(down_at(odd[2], "wd1"))
        hg.extend(odd[3](f"hg{r}", [P, ROW]) for r in range(2, 4))
        esilu = [odd[3](f"esilu{e}", [P, IT, CAP]) for e in range(2)]
        for step in range(3):
            assert odd[step].at <= gu_at + (step + 1) * GU_STEP * 2 * KC * P * 4
        assert odd[3].at <= fore.at, (odd[3].at - base, fore.at - base)

        keep = Place(fore.at)
        sdh = keep("sdh", [P, KT, D], F32R)
        sdl = keep("sdl", [P, KT, D], F32R)
        gw2_at = keep.at
        gw2 = keep("gw2", [P, KC, 2 * E], F32R)
        lsb = keep("lsb", [P, CH])
        fold = keep("fold", [P, E])
        vsum = keep("vsum", [P, 2, KC, BPT])
        hh = keep("hh", [P, KC, CH], F32R)
        hl = keep("hl", [P, KC, CH], F32R)
        h32 = keep("h32", [P, 2, CH])
        h32_end = keep.at
        prod = keep("prod", [P, 2, CH])
        outst = keep("outst", [P, 2, D])
        hrow_at = keep.at
        hrow = keep("hrow", [P, J, ROW])
        qT = keep("qT", [P, KC, B])
        qnT = keep("qnT", [P, KC, B])
        qnT_end = keep.at
        ident = keep("ident", [P, P])
        b2c = keep("b2c", [P, KC])
        b3c = keep("b3c", [P, KC])
        tokrank = keep("tokrank", [P, T // P])
        top = keep("top", [P, J, 8])
        pick = keep("pick", [P, J, 8])
        z_at = keep.at
        z = keep("z", [P, J, E])
        zx = keep("zx", [P, J, E + 2])
        marked = keep("marked", [P, J, E + 2])
        ez = keep("ez", [P, J, E])
        ranks = keep("ranks", [P, J, E])
        ssum = keep("ssum", [P, J])
        rsum = keep("rsum", [P, J])
        cand = keep("cand", [E, CAP + CH])
        cand_end = keep.at
        first = keep("first", [E, CAP])
        slot_no = keep("slot_no", [NP, P])
        firstp = keep("firstp", [NP, P])
        slotp = keep("slotp", [NP, P])
        idx_pair = keep("idx_pair", [P, NP], I32)
        idx_hi = keep("idx_hi", [CAP, NP], I32)
        gidx = [keep(f"gidx{s}", [P, 1], I32) for s in range(8)]
        sidx = [keep(f"sidx{s}", [CAP, 1], I32) for s in range(8)]
        x_at = keep.at
        x32 = keep("x32", [P, 2 * J * D])
        a_at = keep.at
        ah = keep("ah", [P, KT, CH], F32R)
        al = keep("al", [P, NT, CH], F32R)

        late = Place(gw2_at)
        hgt = [late(f"hgt{r}", [P, KC, P]) for r in range(2)]
        ysc = [late(f"ysc{r}", [P, D]) for r in range(4)]
        wd.append(down_at(late, "wd2"))
        assert late.at <= h32_end
        rows_at = Place(hrow_at)
        z_on, x_on = Place(z_at), Place(x_at)
        wg.append([rows_at("wg2_0", [P, KC * I]), x_on("wg2_1", [P, KC * I])])
        wu.append([rows_at("wu2_0", [P, KC * I]), z_on("wu2_1", [P, KC * I])])
        assert rows_at.at <= qnT_end and x_on.at <= x_at + J * D * 4 and z_on.at <= cand_end and NCH % 2 == 0

        def weights_slot(p, q):
            return p if isinstance(p, int) and p < 3 else (q + 1) % 2

        def before_in_slot(p):
            return p - 3 if isinstance(p, int) and p < 5 else p - 2

        st = Place(a_at)
        stage = [st(f"stage{s}", [P, 4 * D]) for s in range(3)]
        assert st.at <= base + arena_bytes
        cs = Place(x_at + J * D * 4)
        w3s = cs("w3s", [P, QC, D])
        conds = cs("conds", [B, Q])
        condT = cs("condT", [P, QC, B])
        assert cs.at <= a_at
        gws = cs("gws", [E, D])
        assert cs.at <= a_at
        zrows = hrow[0:CAP, 0, :]

        bank = [ctx.enter_context(nc.psum_tensor(f"bank{i}", [P, 512], F32)) for i in range(8)]

        class Sems:
            cond_loaded = sem("cond_loaded")
            bias_loaded = sem("bias_loaded")
            gate_loaded = sem("gate_loaded")
            x_loaded = sem("x_loaded")
            zero_rows = sem("zero_rows")
            pads_stored = sem("pads_stored")
            consts_ident = sem("consts_ident")
            slotno_ready = sem("slotno_ready")
            presets = sem("presets")
            condT_filled = sem("condT_filled")
            condT_ready = sem("condT_ready")
            q_filled = sem("q_filled")
            q_ready = sem("q_ready")
            gateT_filled = sem("gateT_filled")
            stage_split_h = sem("stage_split_h")
            w2l_ready = sem("w2l_ready")
            stage_split_l = sem("stage_split_l")
            xs_ready = sem("xs_ready")
            gw2_ready = sem("gw2_ready")
            fold_ready = sem("fold_ready")
            vsum_step = sem("vsum_step")
            xt_filled = sem("xt_filled")
            xm_ready = sem("xm_ready")
            xmh_ready = sem("xmh_ready")
            xml_ready = sem("xml_ready")
            cond_filled = sem("cond_filled")
            cond_taken = sem("cond_taken")
            hh_ready = sem("hh_ready")
            hl_ready = sem("hl_ready")
            rows_filled = sem("rows_filled")
            rows_taken = sem("rows_taken")
            lraw_filled = sem("lraw_filled")
            lraw_taken = sem("lraw_taken")
            logits_filled = sem("logits_filled")
            route_step = sem("route_step")
            z_ready = sem("z_ready")
            exp_ready = sem("exp_ready")
            ranks_ready = sem("ranks_ready")
            scores_ready = sem("scores_ready")
            table_stored = sem("table_stored")
            ranksT_filled = sem("ranksT_filled")
            merge_step = sem("merge_step")
            gu_filled = sem("gu_filled")
            silu_ready = sem("silu_ready")
            prod_ready = sem("prod_ready")
            ah_ready = sem("ah_ready")
            al_ready = sem("al_ready")
            down_filled = sem("down_filled")
            down_taken = sem("down_taken")
            rank_step = sem("rank_step")
            slots_filled = sem("slots_filled")
            slots_ready = sem("slots_ready")
            idx_copied = sem("idx_copied")
            rowsT_filled = sem("rowsT_filled")
            rowsT_ready = sem("rowsT_ready")
            egate_filled = sem("egate_filled")
            esilu_ready = sem("esilu_ready")
            eact_ready = sem("eact_ready")
            edown_filled = sem("edown_filled")
            y_ready = sem("y_ready")
            scattered = sem("scattered")
            passed = sem("passed")

        stage_loaded = [sem(f"stage_loaded{s}") for s in range(3)]
        out_stored = [sem(f"out_stored{s}") for s in range(2)]
        gathered = [sem(f"gathered{s}") for s in range(4)]
        LANES = 5
        LOADS = 8 + 2 * IT
        lane_loaded = [sem(f"lane_loaded{n}") for n in range(LANES)]
        s = Sems

        def wait(eng, semaphore, value):
            if isinstance(value, int) and value <= 0:
                return
            eng.wait_ge(semaphore, value)

        def of_slot(each, ring, p, q):
            return each // ring * p + each - each // ring * q

        def lane_count(p, k):
            return 16 * len(range(k % LANES, LOADS, LANES)) * p + 16 * (k // LANES)

        def wait_load(eng, p, k):
            eng.wait_ge(lane_loaded[k % LANES], lane_count(p, k) + 16)

        def wait_apart(eng, semaphore, value):
            if isinstance(value, int):
                wait(eng, semaphore, value)
            else:
                eng.wait_ge(semaphore, value)
                eng.sem_inc(s.passed, 1)

        w2v = W2.rearrange("(kc p) o -> p kc o", p=P)
        sgv = sw_gate.rearrange("(kc p) i -> p kc i", p=P)
        suv = sw_up.rearrange("(kc p) i -> p kc i", p=P)
        sdv = sw_down[0:NT * P, :].rearrange("(k p) o -> p k o", p=P)

        def stage_view(n, k, w):
            return stage[n % 3][:, 0:k * w].rearrange("p (k w) -> p k w", k=k)

        pieces = [([(w2v, stage_view(0, KC, D))], [(w2h[:, :, :], w2l[:, :, :], stage_view(0, KC, D))])]
        for src, at in ((sgv, 0), (suv, 1)):
            for k0 in (0, 2):
                v = stage_view(len(pieces), 2, IS)
                whole = [gu[:, at:2 * NT:2, half, k0:k0 + 2, :] for half in range(2)]
                tail = [gu[:, 2 * NT, half, k0:k0 + 2, at * TAIL:(at + 1) * TAIL] for half in range(2)]
                pieces.append(([(src[:, k0:k0 + 2, :], v)],
                               [(whole[0], whole[1], v[:, :, 0:NT * P].rearrange("p k (t c) -> p t k c", c=P)),
                                (tail[0], tail[1], v[:, :, NT * P:IS])]))
        v = stage_view(len(pieces), 3, D)
        pieces.append(([(sdv[:, 0:3, :], v)], [(sdh[:, 0:3, :], sdl[:, 0:3, :], v)]))
        v = stage_view(len(pieces), 3, D)
        pieces.append(([(sdv[:, 3:NT, :], v[:, 0:NT - 3, :]), (sw_down[NT * P:IS, :], v[0:TAIL, NT - 3, :]),
                        (sw_down[NT * P:IS, :], v[TAIL:P, NT - 3, :])],
                       [(sdh[:, 3:NT + 1, :], sdl[:, 3:NT + 1, :], v)]))
        splits_before = [sum(len(p[1]) for p in pieces[:n]) for n in range(len(pieces) + 1)]
        loads_before = [sum(len(p[0]) for q, p in enumerate(pieces[:n]) if q % 3 == (n - 1) % 3)
                        for n in range(1, len(pieces) + 1)]
        l_before = [n - len(pieces[0][1]) for n in splits_before]
        GU_SPLIT, SD_SPLIT = l_before[5], l_before[7]

        def x_tile(n, j):
            return x32[:, bass.ds((n % 2) * (J * D) + j * D, D)]

        def x_chunk(n):
            return x32[:, bass.ds((n % 2) * (J * D), J * D)]

        def down_bank(j, last):
            return bank[(5, 4, 7, 5)[j]] if last else bank[3 + j % 2]

        def xm_tile(t, j):
            return t[:, :, j * P:(j + 1) * P]

        block = ctx.enter_context(nc.Block())

        @block.sync
        def _(sp):
            def load_x(n):
                wait(sp, s.down_taken, J * (n - 1))
                sp.dma_start(x_chunk(n).rearrange("p (j d) -> p j d", j=J),
                             xf[bass.ds(n * CH, CH), :].rearrange("(j p) d -> p j d", p=P)).then_inc(s.x_loaded, 16)

            def store_rows(n):
                sp.wait_ge(s.q_ready, 1)
                sp.wait_ge(s.scores_ready, n + 1)
                sp.wait_ge(s.rows_taken, KC * (n + 1))
                sp.dma_start(table[bass.ds(n * CH, CH), :].rearrange("(j p) r -> p j r", p=P),
                             hrow[:, :, :]).then_inc(s.table_stored, 16)

            def store_out(c, j):
                sp.wait_ge(s.down_taken, J * c + j + 1)
                sp.dma_start(of[bass.ds(c * CH + j * P, P), :], outst[:, j % 2, :]).then_inc(out_stored[j % 2], 16)

            def chunk(c):
                load_x(c + 1)
                store_rows(c)
                for j in range(J):
                    store_out(c, j)

            sp.dma_start(conds[:, :], cond).then_inc(s.cond_loaded, 16)
            sp.dma_start(w3s[:, :, :], W3.rearrange("(k p) o -> p k o", p=P)).then_inc(s.cond_loaded, 16)
            sp.dma_start(x32[:, 0:J * D].rearrange("p (j d) -> p j d", j=J),
                         xf[0:CH, :].rearrange("(j p) d -> p j d", p=P)).then_inc(s.x_loaded, 16)
            with nc.allow_non_contiguous_dma(reason="two vectors of 512 elements, once"):
                sp.dma_start(b3c[:, :], b3.rearrange("(k p) -> p k", p=P)).then_inc(s.bias_loaded, 16)
                sp.dma_start(b2c[:, :], b2.rearrange("(k p) -> p k", p=P)).then_inc(s.bias_loaded, 16)
            sp.dma_start(gws[:, :], gate_w).then_inc(s.gate_loaded, 16)
            sp.wait_ge(s.zero_rows, 1)
            sp.dma_start(table[T:T + CAP, :], zrows).then_inc(s.pads_stored, 16)
            sp.dma_start(of[T:T + CAP, :], zrows[:, 0:D]).then_inc(s.pads_stored, 16)
            for n, (loads, _) in enumerate(pieces):
                if n == 3:
                    sp.wait_ge(s.w2l_ready, 1)
                elif n > 3:
                    sp.wait_ge(s.stage_split_l, l_before[n - 2])
                for src, dst in loads:
                    sp.dma_start(dst, src).then_inc(stage_loaded[n % 3], 16)
            sp.wait_ge(s.q_ready, 1)
            sp.wait_ge(s.gateT_filled, 1)
            chunk(0)
            with sp.Fori(1, NCH - 1) as c:
                chunk(c)

            def pairs(w, how, **kw):
                return w.rearrange(how, two=2, **kw)
            gv = pairs(w_gate, "(two e) (p kc) n -> e p two (kc n)", kc=KC)
            uv = pairs(w_up, "(two e) (p kc) n -> e p two (kc n)", kc=KC)
            dv = w_down.rearrange("(two e) i d -> e i two d", two=2)

            def load(p, k, dst, src):
                wait_apart(sp, lane_loaded[k % LANES], lane_count(p, k))
                sp.dma_start(dst, src).then_inc(lane_loaded[k % LANES], 16)

            def load_halves(p, k, w, src, e):
                half = KC * I // 2
                for h in range(2):
                    cols = slice(h * half, (h + 1) * half)
                    load(p, k + h, w[:, cols], src[bass.ds(p, 1), :, e, cols].rearrange("o p n -> (o p) n"))

            def load_gate(p, q, e):
                load_halves(p, 4 * e, wg[weights_slot(p, q)][e], gv, e)

            def load_up(p, q, e):
                load_halves(p, 4 * e + 2, wu[weights_slot(p, q)][e], uv, e)

            def load_down(p, q):
                for e in range(2):
                    w = wd[weights_slot(p, q)][e]
                    if not isinstance(p, int) or p > 2:
                        wait_apart(sp, s.edown_filled, 2 * before_in_slot(p) + e + 1)
                    for it in range(IT):
                        m = ITAIL if it == IT - 1 else P
                        load(p, 8 + IT * e + it, w[0:m, it, :],
                             dv[bass.ds(p, 1), it * P:it * P + m, e, :].rearrange("o p d -> (o p) d"))

            def load_pair(p, q):
                for e in range(2):
                    if not isinstance(p, int) or p > 2:
                        wait_apart(sp, s.egate_filled, 2 * before_in_slot(p) + e + 1)
                    load_gate(p, q, e)
                    load_up(p, q, e)
                load_down(p, q)

            sp.wait_ge(s.cond_filled, KC * NCH)
            for e in range(2):
                load_gate(0, 0, e)
                load_up(0, 0, e)
            store_rows(NCH - 1)
            load_down(0, 0)
            sp.wait_ge(s.gu_filled, GT * (NCH - 1) + GU_STEP)
            load_gate(1, 1, 0)
            sp.wait_ge(s.gu_filled, GT * (NCH - 1) + 2 * GU_STEP)
            load_up(1, 1, 0)
            load_gate(1, 1, 1)
            sp.wait_ge(gathered[0], 16)
            load_up(1, 1, 1)
            sp.wait_ge(s.gu_filled, GT * (NCH - 1) + 3 * GU_STEP)
            load_down(1, 1)
            sp.wait_ge(s.gu_filled, GT * NCH)
            sp.wait_ge(s.table_stored, 16 * NCH)
            sp.wait_ge(s.slots_ready, 1)
            load_pair(2, 0)
            load_pair(3, 1)
            store_out(NCH - 1, 0)
            load_pair(4, 0)
            store_out(NCH - 1, 1)
            store_out(NCH - 1, 2)
            store_out(NCH - 1, 3)
            load_pair(5, 1)
            with sp.Fori(3, NP // 2) as i:
                for q in range(2):
                    load_pair(2 * i + q, q)
            for q in range(2):
                sp.wait_ge(out_stored[q], 32 * NCH)
            sp.wait_ge(s.table_stored, 16 * NCH)
            sp.wait_ge(s.pads_stored, 32)
            sp.wait_ge(s.scattered, 32 * NP)

        @block.gpsimd
        def _(pool):
            nc.gpsimd.memset(ident[:, :], 0.0).then_inc(s.consts_ident, 1)
            pool.wait_ge(s.consts_ident, 1)
            nc.gpsimd.affine_select(out=ident[:, :], in_=ident[:, :], compare_op=ALU.not_equal, fill=1.0, base=0,
                                    pattern=[[-1, P]], channel_multiplier=1).then_inc(s.consts_ident, 1)
            nc.gpsimd.iota(tokrank[:, :], pattern=[[-P, T // P]], base=T, channel_multiplier=-1,
                           allow_small_or_imprecise_dtypes=True).then_inc(s.slotno_ready, 1)
            nc.gpsimd.iota(slot_no[:, :], pattern=[[0, 2], [1, CAP]], base=0, channel_multiplier=0,
                           allow_small_or_imprecise_dtypes=True).then_inc(s.slotno_ready, 1)

            (h_part, l_part, src), = pieces[0][1]
            pool.wait_ge(s.stage_split_h, 1)
            nc.gpsimd.tensor_tensor(l_part, src, h_part.bitcast(F32), ALU.subtract).then_inc(s.w2l_ready, 1)

            AHEAD = 6

            def gather(p, q):
                wait(pool, s.scattered, 32 * (p - 7))
                nc.gpsimd.tensor_copy(gidx[q][:, :], idx_pair[:, bass.ds(p, 1)])
                nc.gpsimd.tensor_copy(sidx[q][:, :], idx_hi[:, bass.ds(p, 1)]).then_inc(s.idx_copied, 1)
                wait(pool, s.y_ready, p - 3)
                wait_apart(pool, s.idx_copied, p + 1)
                nc.gpsimd.indirect_dma_start(
                    out=hg[q % 4][:, :], out_offset=None, in_=table,
                    in_offset=bass.IndirectOffsetOnAxis(ap=gidx[q][:, :], axis=0)).then_inc(gathered[q % 4], 16)

            def scatter(p, q):
                for e, idx in ((0, gidx[q][0:CAP, :]), (1, sidx[q][:, :])):
                    if e == 0:
                        pool.wait_ge(s.y_ready, p + 1)
                    wait_apart(pool, s.scattered, 32 * p + 16 * e)
                    nc.gpsimd.indirect_dma_start(
                        out=of, out_offset=bass.IndirectOffsetOnAxis(ap=idx, axis=0),
                        in_=ysc[q % 4][e * CAP:(e + 1) * CAP, :], in_offset=None,
                        compute_op=ALU.add).then_inc(s.scattered, 16)

            pool.wait_ge(s.slots_ready, 1)
            pool.wait_ge(s.table_stored, 16 * NCH)
            pool.wait_ge(s.pads_stored, 32)
            pool.wait_ge(s.cond_filled, KC * NCH)
            gather(0, 0)
            gather(1, 1)
            pool.wait_ge(s.gu_filled, GT * NCH)
            for p in range(2, AHEAD):
                gather(p, p)
            for q in range(2):
                pool.wait_ge(out_stored[q], 32 * NCH)
            for p in range(8):
                scatter(p, p)
                gather(p + AHEAD, (p + AHEAD) % 8)
            with pool.Fori(1, NP // 8 - 1) as i:
                for q in range(8):
                    scatter(8 * i + q, q)
                    gather(8 * i + q + AHEAD, (q + AHEAD) % 8)
            for p in range(NP - 8, NP):
                scatter(p, p % 8)
                if p + AHEAD < NP:
                    gather(p + AHEAD, (p + AHEAD) % 8)
            pool.wait_ge(s.scattered, 32 * NP)

        @block.scalar
        def _(act):
            def copy(o, i):
                return nc.scalar.activation(o, i, ACT.Copy)

            def copy_x(n, j):
                if j == 0:
                    act.wait_ge(s.x_loaded, 16 * (n + 1))
                wait(act, s.xt_filled, J * n + j - 1)
                copy(xs[:, j % 2, :], x_tile(n, j)).then_inc(s.xs_ready, 1)

            def split_xm(n, j):
                if j == 0:
                    wait(act, s.cond_filled, KC * n)
                act.wait_ge(s.xm_ready, J * n + j + 1)
                copy(xm_tile(xmh, j), xm[:, j % 2, :].rearrange("p (k t) -> p k t", k=KC)).then_inc(s.xmh_ready, 1)

            def take_cond(n, oc):
                act.wait_ge(s.cond_filled, KC * n + oc + 1)
                if oc >= 2:
                    act.wait_ge(s.rows_filled, KC * n + oc - 1)
                    act.wait_ge(s.hl_ready, KC * n + oc - 1)
                else:
                    wait(act, s.rows_filled, KC * n)
                    wait(act, s.hl_ready, KC * n)
                if oc == 0:
                    wait(act, s.gu_filled, GT * n)
                nc.scalar.activation(h32[:, oc % 2, :], bank[5 + oc % 2][:, :], ACT.Relu,
                                     bias=b2c[:, oc:oc + 1]).then_inc(s.cond_taken, 1)
                act.wait_ge(s.cond_taken, KC * n + oc + 1)
                copy(hh[:, oc, :], h32[:, oc % 2, :]).then_inc(s.hh_ready, 1)

            def take_rows(n, oc):
                if oc == 0:
                    wait(act, s.table_stored, 16 * n)
                act.wait_ge(s.rows_filled, KC * n + oc + 1)
                copy(hrow[:, :, oc * P:(oc + 1) * P],
                     bank[2 * (oc % 2)][:, :].rearrange("p (j f) -> p j f", j=J)).then_inc(s.rows_taken, 1)

            def take_lraw(n):
                act.wait_ge(s.lraw_filled, n + 1)
                wait(act, s.logits_filled, n)
                copy(lsb[:, :], bank[1][:, :]).then_inc(s.lraw_taken, 1)

            def exp_scores(c):
                act.wait_ge(s.z_ready, c + 1)
                nc.scalar.activation(ez[:, :, :], z[:, :, :], ACT.Exp).then_inc(s.exp_ready, 1)

            def silu(c, i):
                t = min(2 * i, GT - 1)
                act.wait_ge(s.gu_filled, GT * c + t + 1)
                wait(act, s.al_ready, KT * c + max(i - 1, 0))
                m = TAIL if i == NT else P
                nc.scalar.activation(prod[0:m, i % 2, :], bank[t % 3][0:m, :], ACT.Silu).then_inc(s.silu_ready, 1)

            def split_a(c, i):
                if i == 0:
                    wait(act, s.down_filled, J * c)
                act.wait_ge(s.prod_ready, KT * c + i + 1)
                m = TAIL if i == NT else P
                copy(ah[0:m, i, :], prod[0:m, i % 2, :]).then_inc(s.ah_ready, 1)

            def take_rowsT(p, q):
                act.wait_ge(s.rowsT_filled, p + 1)
                wait(act, s.egate_filled, 2 * (p - 1))
                copy(hgt[q][:, :, :], bank[6 + q][:, :].rearrange("p (k t) -> p k t", k=KC)).then_inc(s.rowsT_ready, 1)

            def chunk(c, last):
                n = c + 1
                silu(c, 0)
                if not last:
                    copy_x(n, 0)
                    copy_x(n, 1)
                exp_scores(c)
                silu(c, 1)
                split_a(c, 0)
                silu(c, 2)
                split_a(c, 1)
                if not last:
                    copy_x(n, 2)
                    copy_x(n, 3)
                    split_xm(n, 0)
                    split_xm(n, 1)
                silu(c, 3)
                split_a(c, 2)
                if not last:
                    split_xm(n, 2)
                    split_xm(n, 3)
                silu(c, 4)
                split_a(c, 3)
                if last:
                    split_a(c, 4)
                    take_rowsT(0, 0)
                    silu(c, 5)
                else:
                    silu(c, 5)
                    split_a(c, 4)
                split_a(c, 5)
                if not last:
                    adaln(n)

            def adaln(n):
                take_cond(n, 0)
                if isinstance(n, int) and n == 0:
                    split_piece(4)
                take_cond(n, 1)
                take_rows(n, 0)
                take_cond(n, 2)
                take_rows(n, 1)
                take_cond(n, 3)
                take_rows(n, 2)
                take_rows(n, 3)
                take_lraw(n)

            act.wait_ge(s.condT_filled, 1)
            copy(condT[:, :, :], bank[5][:, 0:QC * B].rearrange("p (k b) -> p k b", k=QC)).then_inc(s.condT_ready, 1)
            copy_x(0, 0)
            copy_x(0, 1)
            act.wait_ge(s.bias_loaded, 32)
            act.wait_ge(s.q_filled, 1)
            for fc in range(KC):
                last = nc.scalar.activation(qT[:, fc, :], bank[6][:, fc * B:(fc + 1) * B], ACT.Relu,
                                            bias=b3c[:, fc:fc + 1])
            last.then_inc(s.q_ready, 1)

            def split_piece(n):
                act.wait_ge(stage_loaded[n % 3], 16 * loads_before[n])
                for h_part, _, src in pieces[n][1]:
                    copy(h_part, src).then_inc(s.stage_split_h, 1)

            split_piece(0)
            copy_x(0, 2)
            copy_x(0, 3)
            for j in range(J):
                split_xm(0, j)
            act.wait_ge(s.gateT_filled, 1)
            copy(gw2[:, :, 0:E], bank[7][:, 0:KC * E].rearrange("p (k e) -> p k e", k=KC)).then_inc(s.gw2_ready, 1)
            split_piece(1)
            split_piece(2)
            split_piece(3)
            act.wait_ge(s.pads_stored, 32)
            adaln(0)
            split_piece(5)
            split_piece(6)
            chunk(0, False)
            with act.Fori(1, NCH - 1) as c:
                chunk(c, False)
            chunk(NCH - 1, True)

            def esilu_of(p, e):
                act.wait_ge(s.egate_filled, 2 * p + e + 1)
                wait(act, s.eact_ready, 2 * p)
                g = bank[2 * e]
                nc.scalar.activation(esilu[e][:, 0:IT - 1, :],
                                     g[:, 0:(IT - 1) * CAP].rearrange("p (i t) -> p i t", t=CAP), ACT.Silu)
                nc.scalar.activation(esilu[e][0:ITAIL, IT - 1, :], g[0:ITAIL, (IT - 1) * CAP:IT * CAP],
                                     ACT.Silu).then_inc(s.esilu_ready, 1)

            def pair(p, q, last):
                esilu_of(p, 0)
                if not last:
                    take_rowsT(p + 1, 1 - q)
                esilu_of(p, 1)

            pair(0, 0, False)
            pair(1, 1, False)
            with act.Fori(1, NP // 2 - 1) as i:
                for q in range(2):
                    pair(2 * i + q, q, False)
            pair(NP - 2, 0, False)
            pair(NP - 1, 1, True)

        @block.vector
        def _(dve):
            def lower(o, full, high):
                return nc.vector.tensor_tensor(o, full, high.bitcast(F32), ALU.subtract)

            def take_xt(n, j):
                xt = bank[3 + j % 2][:, :].rearrange("p (k b t) -> p k b t", k=KC, b=BPT)
                xm4 = xm[:, j % 2, :].rearrange("p (k b t) -> p k b t", k=KC, b=BPT)
                batches = bass.ds(n * BPC + j * BPT, BPT)
                steps = 3 * (J * n + j)
                wait(dve, s.xm_ready, J * n + j)
                wait(dve, s.xml_ready, J * n + max(j - 1, 0))
                dve.wait_ge(s.xt_filled, J * n + j + 1)
                nc.vector.reduce_sum(vsum[:, 0, :, :], xt, AX).then_inc(s.vsum_step, 1)
                nc.vector.tensor_tensor(xm4, xt, qnT[:, :, batches].unsqueeze(3).to_broadcast([P, KC, BPT, N]),
                                        ALU.mult).then_inc(s.vsum_step, 1)
                dve.wait_ge(s.vsum_step, steps + 2)
                nc.vector.tensor_tensor(vsum[:, 1, :, :], vsum[:, 0, :, :], qT[:, :, batches],
                                        ALU.mult).then_inc(s.vsum_step, 1)
                dve.wait_ge(s.vsum_step, steps + 3)
                nc.vector.tensor_tensor(xm4, xm4, vsum[:, 1, :, :].unsqueeze(3).to_broadcast([P, KC, BPT, N]),
                                        ALU.add).then_inc(s.xm_ready, 1)

            def split_xm(n, j):
                dve.wait_ge(s.xmh_ready, J * n + j + 1)
                lower(xm_tile(xml, j), xm[:, j % 2, :].rearrange("p (k t) -> p k t", k=KC),
                      xm_tile(xmh, j)).then_inc(s.xml_ready, 1)

            def split_h(n, oc):
                dve.wait_ge(s.hh_ready, KC * n + oc + 1)
                lower(hl[:, oc, :], h32[:, oc % 2, :], hh[:, oc, :]).then_inc(s.hl_ready, 1)

            def product(c, i):
                t = min(2 * i + 1, GT - 1)
                dve.wait_ge(s.gu_filled, GT * c + t + 1)
                dve.wait_ge(s.silu_ready, KT * c + i + 1)
                m, up0 = (TAIL, TAIL) if i == NT else (P, 0)
                nc.vector.tensor_tensor(prod[0:m, i % 2, :], bank[t % 3][up0:up0 + m, :], prod[0:m, i % 2, :],
                                        ALU.mult).then_inc(s.prod_ready, 1)

            def split_a(c, i):
                dve.wait_ge(s.ah_ready, KT * c + i + 1)
                if i < NT:
                    lower(al[:, i, :], prod[:, i % 2, :], ah[:, i, :]).then_inc(s.al_ready, 1)
                else:
                    lower(ah[TAIL:P, NT, :], prod[0:TAIL, i % 2, :], ah[0:TAIL, NT, :]).then_inc(s.al_ready, 1)

            def take_down(c, j, last):
                dve.wait_ge(s.down_filled, J * c + j + 1)
                wait(dve, out_stored[j % 2], 16 * (2 * c + j // 2))
                nc.vector.tensor_tensor(outst[:, j % 2, :], down_bank(j, last)[:, :], x_tile(c, j),
                                        ALU.add).then_inc(s.down_taken, 1)

            ROUTE_STEPS = 6

            def route(c):
                lg = bank[7][:, 0:J * E].rearrange("p (j e) -> p j e", j=J)
                step = [ROUTE_STEPS * c]

                def link(op):
                    step[0] = step[0] + 1
                    op.then_inc(s.route_step, 1)
                    dve.wait_ge(s.route_step, step[0])

                wait_apart(dve, s.logits_filled, c + 1)
                for j in range(J):
                    op = nc.vector.max(top[:, j, :], lg[:, j, :])
                link(op)
                nc.vector.tensor_tensor(pick[:, :, 0:TOPK], top[:, :, 0:TOPK],
                                        top[:, :, 0:1].to_broadcast([P, J, TOPK]), ALU.subtract)
                link(nc.vector.tensor_tensor(z[:, :, :], lg, top[:, :, 0:1].to_broadcast([P, J, E]), ALU.subtract))
                nc.vector.tensor_scalar(zx[:, :, 0:E], z[:, :, :], EXP_UNDERFLOW, None, ALU.max).then_inc(s.z_ready, 1)
                nc.vector.tensor_scalar(pick[:, :, 0:TOPK], pick[:, :, 0:TOPK], EXP_UNDERFLOW, None,
                                        ALU.max).then_inc(s.route_step, 1)
                step[0] = step[0] + 1
                wait_apart(dve, s.route_step, step[0])
                for j in range(J):
                    op = nc.vector.match_replace(marked[:, j, :], pick[:, j, :], zx[:, j, :], TAKEN)
                link(op)
                for j in range(J):
                    op = nc.vector.tensor_scalar(ranks[:, j, :], marked[:, j, 0:E], TAKEN - 1.0,
                                                 tokrank[:, bass.ds(c * J + j, 1)], ALU.is_ge, ALU.mult)
                op.then_inc(s.ranks_ready, 1)
                product(c, 0)
                dve.wait_ge(s.exp_ready, c + 1)
                link(nc.vector.reduce_sum(ssum[:, :], ez[:, :, :], AX))
                link(nc.vector.reciprocal(rsum[:, :], ssum[:, :]))
                wait(dve, s.table_stored, 16 * c)
                nc.vector.tensor_tensor(hrow[:, :, D:ROW], ez[:, :, :],
                                        rsum[:, :].unsqueeze(2).to_broadcast([P, J, E]),
                                        ALU.mult).then_inc(s.scores_ready, 1)

            MERGE_STEPS = 1 + 2 * NR

            def take_ranksT(c):
                dve.wait_ge(s.ranksT_filled, c + 1)
                nc.vector.tensor_copy(cand[:, CAP:CAP + CH], bank[7][0:E, :]).then_inc(s.merge_step, 1)

            def merge(c, r):
                eight = first[:, 8 * r:8 * r + 8]
                wait_apart(dve, s.merge_step, MERGE_STEPS * c + 1 + 2 * r)
                nc.vector.max(eight, cand[:, :]).then_inc(s.merge_step, 1)
                wait_apart(dve, s.merge_step, MERGE_STEPS * c + 2 + 2 * r)
                if r < NR - 1:
                    nc.vector.match_replace(cand[:, :], eight, cand[:, :], 0.0).then_inc(s.merge_step, 1)
                else:
                    nc.vector.tensor_copy(cand[:, 0:CAP], first[:, :]).then_inc(s.merge_step, 1)

            def chunk(c):
                n = c + 1
                route(c)
                product(c, 1)
                split_a(c, 0)
                product(c, 2)
                split_a(c, 1)
                take_xt(n, 0)
                take_xt(n, 1)
                split_xm(n, 0)
                split_xm(n, 1)
                product(c, 3)
                split_a(c, 2)
                take_xt(n, 2)
                take_xt(n, 3)
                split_xm(n, 2)
                split_xm(n, 3)
                product(c, 4)
                split_a(c, 3)
                product(c, 5)
                split_a(c, 4)
                split_a(c, 5)
                take_ranksT(c)
                for r in range(KC):
                    merge(c, r)
                    split_h(n, r)
                for j in range(J):
                    take_down(c, j, False)
                    merge(c, KC + j)

            def last_chunk(c):
                route(c)
                take_ranksT(c)
                merge(c, 0)
                merge(c, 1)
                product(c, 1)
                split_a(c, 0)
                merge(c, 2)
                merge(c, 3)
                merge(c, 4)
                product(c, 2)
                split_a(c, 1)
                merge(c, 5)
                merge(c, 6)
                merge(c, 7)
                slot_ranks()
                product(c, 3)
                split_a(c, 2)
                slot_rows()
                product(c, 4)
                split_a(c, 3)
                product(c, 5)
                split_a(c, 4)
                split_a(c, 5)

            def slot_ranks():
                done = [0]

                def link(op):
                    done[0] += 1
                    op.then_inc(s.rank_step, 1)
                    dve.wait_ge(s.rank_step, done[0])

                dve.wait_ge(s.merge_step, MERGE_STEPS * NCH)
                for half in range(2):
                    op = nc.vector.tensor_copy(firstp[:, half * CAP:(half + 1) * CAP], first[half * NP:(half + 1) * NP, :])
                link(op)
                link(nc.vector.scalar_tensor_tensor(out=slotp[:, :], in0=firstp[:, :], scalar=0.0, in1=slot_no[:, :],
                                                    op0=ALU.is_equal, op1=ALU.mult))
                nc.vector.tensor_tensor(slotp[:, :], slotp[:, :], firstp[:, :], ALU.subtract).then_inc(s.rank_step, 1)

            def slot_rows():
                dve.wait_ge(s.slots_filled, 1)
                nc.vector.tensor_scalar(idx_pair[:, :], bank[5][:, 0:NP], float(T), None, ALU.add)
                nc.vector.tensor_scalar(idx_hi[:, :], bank[5][0:CAP, NP:2 * NP], float(T), None,
                                        ALU.add).then_inc(s.slots_ready, 1)

            nc.vector.memset(hrow[0:CAP, 0, :], 0.0).then_inc(s.zero_rows, 1)
            nc.vector.memset(cand[:, 0:CAP], 0.0).then_inc(s.presets, 1)
            nc.vector.memset(pick[:, :, TOPK:8], SENTINEL).then_inc(s.presets, 1)
            nc.vector.memset(zx[:, :, E:E + 2], SENTINEL).then_inc(s.presets, 1)
            dve.wait_ge(s.presets, 3)
            dve.wait_ge(s.consts_ident, 2)
            nc.vector.tensor_copy(fold[0:E, :], ident[0:E, 0:E]).then_inc(s.fold_ready, 1)
            nc.vector.tensor_copy(fold[E:P, :], ident[E:P, E:P]).then_inc(s.fold_ready, 1)
            dve.wait_ge(s.slotno_ready, 2)

            def split_piece(n):
                for k, (_, l_part, src) in enumerate(pieces[n][1]):
                    dve.wait_ge(s.stage_split_h, splits_before[n] + k + 1)
                    high = pieces[n][1][k][0]
                    lower(l_part, src, high).then_inc(s.stage_split_l, 1)

            dve.wait_ge(s.q_ready, 1)
            nc.vector.tensor_scalar(qnT[:, :, :], qT[:, :, :], float(N), None, ALU.mult).then_inc(s.presets, 1)
            dve.wait_ge(s.presets, 4)
            for j in range(J):
                take_xt(0, j)
                if j >= 1:
                    split_xm(0, j - 1)
            split_xm(0, J - 1)
            dve.wait_ge(s.gw2_ready, 1)
            lower(gw2[:, :, E:2 * E], bank[7][:, 0:KC * E].rearrange("p (k e) -> p k e", k=KC),
                  gw2[:, :, 0:E]).then_inc(s.gw2_ready, 1)
            split_piece(1)
            split_piece(2)
            split_piece(3)
            split_piece(4)
            for oc in range(KC):
                split_h(0, oc)
            split_piece(5)
            split_piece(6)
            dve.wait_ge(s.pads_stored, 32)
            chunk(0)
            with dve.Fori(1, NCH - 1) as c:
                chunk(c)
            last_chunk(NCH - 1)

            def eproduct(p, q):
                for e in range(2):
                    dve.wait_ge(s.esilu_ready, 2 * p + e + 1)
                    wait(dve, s.edown_filled, 2 * p + e - 1)
                    u = bank[2 * e + 1]
                    nc.vector.tensor_tensor(eact[e][:, 0:IT - 1, :],
                                            u[:, 0:(IT - 1) * CAP].rearrange("p (i t) -> p i t", t=CAP),
                                            esilu[e][:, 0:IT - 1, :], ALU.mult)
                    nc.vector.tensor_tensor(eact[e][0:ITAIL, IT - 1, :], u[0:ITAIL, (IT - 1) * CAP:IT * CAP],
                                            esilu[e][0:ITAIL, IT - 1, :], ALU.mult).then_inc(s.eact_ready, 1)

            def scale_y(p, q):
                dve.wait_ge(s.edown_filled, 2 * (p + 1))
                wait(dve, s.scattered, 32 * (p - 3))
                for e in range(2):
                    rows = slice(e * CAP, (e + 1) * CAP)
                    op = nc.vector.tensor_scalar(ysc[q][rows, :], bank[4 + q % 2][rows, :],
                                                 hg[q][rows, bass.ds(p + D + e * NP, 1)], None, ALU.mult)
                op.then_inc(s.y_ready, 1)

            for p in range(4):
                eproduct(p, p)
                scale_y(p, p)
                if p == 0:
                    take_down(NCH - 1, 0, True)
                elif p == 1:
                    take_down(NCH - 1, 1, True)
                    take_down(NCH - 1, 2, True)
                elif p == 2:
                    take_down(NCH - 1, 3, True)
            with dve.Fori(1, NP // 4) as i:
                for q in range(4):
                    eproduct(4 * i + q, q)
                    scale_y(4 * i + q, q)

        @block.tensor
        def _(pe):
            def three(o, st_h, st_l, mv_h, mv_l, first_mm, last_mm):
                nc.tensor.matmul(o, st_h, mv_h, start=first_mm, stop=False)
                nc.tensor.matmul(o, st_h, mv_l, start=False, stop=False)
                return nc.tensor.matmul(o, st_l, mv_h, start=False, stop=last_mm)

            def transpose_x(n, j):
                pe.wait_ge(s.xs_ready, J * n + j + 1)
                if j < 2:
                    wait(pe, s.down_taken, J * (n - 1))
                else:
                    pe.wait_ge(s.xm_ready, J * n + j - 1)
                for k in range(KC):
                    op = nc.tensor.transpose(bank[3 + j % 2][:, k * P:(k + 1) * P],
                                             xs[:, j % 2, k * P:(k + 1) * P], ident[:, :])
                op.then_inc(s.xt_filled, 1)

            def cond_tile(n, oc):
                if oc == 0:
                    pe.wait_ge(s.xmh_ready, J * (n + 1))
                    pe.wait_ge(s.xml_ready, J * (n + 1))
                if oc >= 2:
                    pe.wait_ge(s.cond_taken, KC * n + oc - 1)
                else:
                    wait(pe, s.cond_taken, KC * n)
                for k in range(KC):
                    cols = slice(oc * P, (oc + 1) * P)
                    op = three(bank[5 + oc % 2][:, :], w2h[:, k, cols], w2l[:, k, cols], xmh[:, k, :], xml[:, k, :],
                               k == 0, k == KC - 1)
                op.then_inc(s.cond_filled, 1)

            def rows_tile(n, oc):
                pe.wait_ge(s.cond_taken, KC * n + oc + 1)
                if oc >= 2:
                    pe.wait_ge(s.rows_taken, KC * n + oc - 1)
                elif oc == 0:
                    wait(pe, s.prod_ready, KT * n)
                for j in range(J):
                    op = nc.tensor.transpose(bank[2 * (oc % 2)][:, j * P:(j + 1) * P],
                                             h32[:, oc % 2, j * P:(j + 1) * P], ident[:, :])
                op.then_inc(s.rows_filled, 1)

            def logits_raw(n):
                pe.wait_ge(s.hh_ready, KC * (n + 1))
                pe.wait_ge(s.hl_ready, KC * (n + 1))
                wait(pe, s.prod_ready, KT * n)
                for k in range(KC):
                    if k == KC - 1:
                        nc.tensor.matmul(bank[1][0:E, :], gw2[:, k, 0:E], hl[:, k, :], start=False, stop=False)
                        op = nc.tensor.matmul(bank[1][:, :], gw2[:, k, :], hh[:, k, :], start=False, stop=True)
                    else:
                        nc.tensor.matmul(bank[1][:, :], gw2[:, k, :], hh[:, k, :], start=(k == 0), stop=False)
                        nc.tensor.matmul(bank[1][0:E, :], gw2[:, k, 0:E], hl[:, k, :], start=False, stop=False)
                op.then_inc(s.lraw_filled, 1)

            def logits(n):
                pe.wait_ge(s.lraw_taken, n + 1)
                wait(pe, s.merge_step, (2 * NR + 1) * (n - 1) + 1 if not (isinstance(n, int) and n == 0) else 0)
                for j in range(J):
                    op = nc.tensor.matmul(bank[7][:, j * E:(j + 1) * E], lsb[:, j * P:(j + 1) * P], fold[:, :],
                                          start=True, stop=True)
                op.then_inc(s.logits_filled, 1)

            def gu_tile(c, t):
                if t == 0:
                    pe.wait_ge(s.hl_ready, KC * (c + 1))
                    pe.wait_ge(s.rows_taken, KC * (c + 1))
                    wait(pe, s.prod_ready, KT * c)
                if t == 1:
                    pe.wait_ge(s.lraw_taken, c + 1)
                if t >= 3:
                    u = t - 3
                    if u % 2 == 0:
                        pe.wait_ge(s.silu_ready, KT * c + u // 2 + 1)
                    else:
                        pe.wait_ge(s.prod_ready, KT * c + u // 2 + 1)
                for k in range(KC):
                    op = three(bank[t % 3][:, :], gu[:, t, 0, k, :], gu[:, t, 1, k, :], hh[:, k, :], hl[:, k, :],
                               k == 0, k == KC - 1)
                op.then_inc(s.gu_filled, 1)

            def ranksT(c):
                wait_apart(pe, s.ranks_ready, c + 1)
                for j in range(J):
                    op = nc.tensor.transpose(bank[7][0:E, j * P:(j + 1) * P], ranks[:, j, :], ident[:, :])
                op.then_inc(s.ranksT_filled, 1)

            def down_tile(c, j, last):
                if j == 0:
                    pe.wait_ge(s.ah_ready, KT * (c + 1))
                    pe.wait_ge(s.al_ready, KT * (c + 1))
                    if isinstance(c, int) and c == 0:
                        pe.wait_ge(s.stage_split_l, SD_SPLIT)
                if last:
                    if j == 0:
                        pe.wait_ge(s.slots_ready, 1)
                    elif j == 1:
                        pe.wait_ge(s.y_ready, 1)
                    elif j == 2:
                        pe.wait_ge(s.rowsT_ready, 2)
                    else:
                        pe.wait_ge(s.y_ready, 2)
                elif j < 2:
                    pe.wait_ge(s.xm_ready, J * (c + 2))
                else:
                    pe.wait_ge(s.down_taken, J * c + j - 1)
                o = down_bank(j, last)[:, :]
                t = slice(j * P, (j + 1) * P)
                for k in range(NT):
                    three(o, ah[:, k, t], al[:, k, t], sdh[:, k, :], sdl[:, k, :], k == 0, False)
                nc.tensor.matmul(o, ah[:, NT, t], sdh[:, NT, :], start=False, stop=False)
                op = nc.tensor.matmul(o, ah[0:TAIL, NT, t], sdl[0:TAIL, NT, :], start=False, stop=True)
                op.then_inc(s.down_filled, 1)

            def chunk(c):
                n = c + 1
                for t in range(GT):
                    gu_tile(c, t)
                    if t == 0 and isinstance(c, int) and c == 0:
                        logits(0)
                    if t == 5:
                        transpose_x(n, 0)
                        transpose_x(n, 1)
                    if t == 7:
                        transpose_x(n, 2)
                        transpose_x(n, 3)
                ranksT(c)
                adaln_head(n)
                down_tile(c, 0, False)
                rows_tile(n, 3)
                down_tile(c, 1, False)
                logits_raw(n)
                down_tile(c, 2, False)
                logits(n)
                down_tile(c, 3, False)

            def rowsT(p, q):
                pe.wait_ge(gathered[q], of_slot(16, 4, p, q))
                wait(pe, s.rowsT_ready, p - 1)
                if isinstance(p, int) and p == 3:
                    pe.wait_ge(s.down_taken, J * (NCH - 1) + 3)
                if isinstance(p, int) and p == 1:
                    pe.wait_ge(s.merge_step, (2 * NR + 1) * (NCH - 1) + 1)
                v = hg[q][:, 0:D].rearrange("t (p k) -> t k p", k=KC)
                for k in range(KC):
                    op = nc.tensor.transpose(bank[6 + q % 2][:, k * P:(k + 1) * P], v[:, k, :], ident[:, :])
                op.then_inc(s.rowsT_filled, 1)

            def last_chunk(c):
                for t in range(GT):
                    gu_tile(c, t)
                    if t == 1:
                        ranksT(c)
                    if t == 8:
                        pe.wait_ge(s.rank_step, 3)
                        nc.tensor.transpose(bank[5][:, 0:NP], slotp[:, :], ident[0:NP, 0:NP])
                        nc.tensor.transpose(bank[5][0:CAP, NP:2 * NP], slotp[:, CAP:P],
                                            ident[0:NP, 0:NP]).then_inc(s.slots_filled, 1)
                    if t == 9:
                        rowsT(0, 0)
            def adaln_head(n):
                cond_tile(n, 0)
                cond_tile(n, 1)
                rows_tile(n, 0)
                cond_tile(n, 2)
                rows_tile(n, 1)
                cond_tile(n, 3)
                rows_tile(n, 2)

            pe.wait_ge(s.consts_ident, 2)
            pe.wait_ge(s.cond_loaded, 32)
            for k in range(QC):
                op = nc.tensor.transpose(bank[5][:, k * B:(k + 1) * B], conds[:, k * P:(k + 1) * P], ident[:, :])
            op.then_inc(s.condT_filled, 1)
            pe.wait_ge(s.condT_ready, 1)
            for fc in range(KC):
                for k in range(QC):
                    op = nc.tensor.matmul(bank[6][:, fc * B:(fc + 1) * B], w3s[:, k, fc * P:(fc + 1) * P],
                                          condT[:, k, :], start=(k == 0), stop=(k == QC - 1))
            op.then_inc(s.q_filled, 1)
            pe.wait_ge(s.gate_loaded, 16)
            for k in range(KC):
                op = nc.tensor.transpose(bank[7][:, k * E:(k + 1) * E], gws[:, k * P:(k + 1) * P], ident[0:E, 0:E])
            op.then_inc(s.gateT_filled, 1)
            for j in range(J):
                transpose_x(0, j)
            pe.wait_ge(s.q_ready, 1)
            pe.wait_ge(s.w2l_ready, 1)
            adaln_head(0)
            rows_tile(0, 3)
            pe.wait_ge(s.gw2_ready, 2)
            logits_raw(0)
            pe.wait_ge(s.fold_ready, 2)
            pe.wait_ge(s.stage_split_l, GU_SPLIT)
            chunk(0)
            with pe.Fori(1, NCH - 1) as c:
                chunk(c)
            last_chunk(NCH - 1)

            def egate(p, q, e):
                if e == 0:
                    pe.wait_ge(s.rowsT_ready, p + 1)
                for k in range(4 * e, 4 * e + 4):
                    wait_load(pe, p, k)
                wait(pe, s.eact_ready, 2 * p)
                if isinstance(p, int) and p == 0:
                    pe.wait_ge(s.prod_ready, KT * NCH - (1 - e))
                    pe.wait_ge(s.down_taken, J * (NCH - 1))
                slot = weights_slot(p, q)
                for w, b in ((wg[slot][e], bank[2 * e]), (wu[slot][e], bank[2 * e + 1])):
                    if isinstance(p, int) and p == 0 and b is bank[1]:
                        pe.wait_ge(s.prod_ready, KT * NCH)
                    for it in range(IT):
                        m = ITAIL if it == IT - 1 else P
                        for k in range(KC):
                            op = nc.tensor.matmul(b[0:m, it * CAP:(it + 1) * CAP],
                                                  w[:, k * I + it * P:k * I + it * P + m],
                                                  hgt[q % 2][:, k, e * CAP:(e + 1) * CAP],
                                                  start=(k == 0), stop=(k == KC - 1))
                op.then_inc(s.egate_filled, 1)

            def edown(p, q, e):
                pe.wait_ge(s.eact_ready, 2 * p + e + 1)
                for k in range(8 + IT * e, 8 + IT * e + IT):
                    wait_load(pe, p, k)
                if e == 0:
                    wait(pe, s.y_ready, p - 1)
                    if isinstance(p, int) and p in (1, 2, 3):
                        pe.wait_ge(s.down_taken, J * (NCH - 1) + (1, 2, 4)[p - 1])
                for it in range(IT):
                    m = ITAIL if it == IT - 1 else P
                    op = nc.tensor.matmul(bank[4 + q % 2][e * CAP:(e + 1) * CAP, :], eact[e][0:m, it, :],
                                          wd[weights_slot(p, q)][e][0:m, it, :], start=(it == 0), stop=(it == IT - 1))
                op.then_inc(s.edown_filled, 1)

            def pair(p, q, last):
                egate(p, q, 0)
                if not last:
                    rowsT(p + 1, (q + 1) % 4)
                egate(p, q, 1)
                edown(p, q, 0)
                edown(p, q, 1)

            pair(0, 0, False)
            down_tile(NCH - 1, 0, True)
            pair(1, 1, False)
            down_tile(NCH - 1, 1, True)
            down_tile(NCH - 1, 2, True)
            pair(2, 2, False)
            down_tile(NCH - 1, 3, True)
            pair(3, 3, False)
            with pe.Fori(1, NP // 4 - 1) as i:
                for q in range(4):
                    pair(4 * i + q, q, False)
            for p in range(NP - 4, NP):
                pair(p, p % 4, p == NP - 1)


_INS = ['x', 'cond_1024', 'L0_cond_W3', 'L0_cond_b3', 'L0_cond_W2', 'L0_cond_b2', 'L0_ffn_gate_w',
        'L0_ffn_w_gate', 'L0_ffn_w_up', 'L0_ffn_w_down', 'L0_ffn_sw_gate', 'L0_ffn_sw_up', 'L0_ffn_sw_down']


def kernel(**inputs):
    import numpy as _np
    import concourse.bacc as _bacc
    from concourse import mybir as _mybir
    from concourse.bass_utils import run_bass_kernel_spmd as _run

    nc = _bacc.Bacc("TRN2", target_bir_lowering=False, num_devices=1)
    arrays, args = {}, []
    for name in _INS:
        a = _np.ascontiguousarray(inputs[name])
        arrays[f"in_{name}_dram"] = a
        args.append(nc.dram_tensor(f"in_{name}_dram", a.shape, _mybir.dt.from_np(a.dtype), kind="ExternalInput").ap())
    b, n, d = inputs['x'].shape
    args.append(nc.dram_tensor("out_0_dram", (b * n + CAP, d), _mybir.dt.float32, kind="ExternalOutput").ap())
    adaln_moe_ffn_kernel(nc, *args)
    r = _run(nc, [arrays], core_ids=[0])
    return r.results[0]["out_0_dram"][:b * n].reshape(b, n, d)
```
